# Optimizing a Trainium2 kernel written in Bass

```python
import numpy as np
import jax
import jax.numpy as jnp

def _softmax(x, axis=-1):
    return jax.nn.softmax(x, axis=axis)

def _gelu(x):
    return jax.nn.gelu(x, approximate=True)

def _silu(x):
    return jax.nn.silu(x)

def _sigmoid(x):
    return jax.nn.sigmoid(x)

def _layernorm(x, axis=-1, eps=1e-05):
    m = jnp.mean(x, axis=axis, keepdims=True)
    v = jnp.var(x, axis=axis, keepdims=True)
    return (x - m) / jnp.sqrt(v + eps)

def _scatter_add(tgt, idx, src, axis=0):
    return tgt.at[idx].add(src)

def _segment_sum(src, seg, n):
    return jax.ops.segment_sum(src, seg, n)
kernel_name = 'mk_sandwich_d1_jaxref_r8_21cedd'

def setup_inputs(seed: int=0):
    np.random.seed(seed)
    _w = jnp.asarray

    def _L0_attn_setup():
        import jax, jax.numpy as jnp
        import numpy as np
        B, S, H_DIM = (2, 256, 256)
        N_HEADS, D_HEAD = (16, 128)
        key = jax.random.key(seed)
        k1, k2, k3 = jax.random.split(key, 3)
        x = jax.random.normal(k1, (B, S, H_DIM), dtype=jnp.float32)
        w_qkv = jax.random.normal(k2, (H_DIM, 3 * N_HEADS * D_HEAD), dtype=jnp.float32) * 0.02
        w_o = jax.random.normal(k3, (N_HEADS * D_HEAD, H_DIM), dtype=jnp.float32) * 0.02
        return {'x': x, 'w_qkv': w_qkv, 'w_o': w_o}
    _L0_attn_in = _L0_attn_setup()

    def _L0_ffn_setup():
        import jax, jax.numpy as jnp
        import numpy as np
        EPS = 1e-08

        def _bit_quant(w):
            scale = jnp.maximum(jnp.mean(jnp.abs(w)), EPS)
            w_ternary = jnp.clip(jnp.round(w / scale), -1.0, 1.0)
            return w + jax.lax.stop_gradient(w_ternary - w)
        key = jax.random.key(seed)
        k = jax.random.split(key, 5)
        emb, dff = (256, 1024)
        B, S = (4, 256)
        x = jax.random.normal(k[0], (B, S, emb), dtype=jnp.float32)
        w1 = jax.random.normal(k[1], (dff, emb), dtype=jnp.float32) * 0.02
        b1 = jax.random.normal(k[2], (dff,), dtype=jnp.float32) * 0.02
        w2 = jax.random.normal(k[3], (emb, dff), dtype=jnp.float32) * 0.02
        b2 = jax.random.normal(k[4], (emb,), dtype=jnp.float32) * 0.02
        return {'x': x, 'w1': w1, 'b1': b1, 'w2': w2, 'b2': b2}
    _L0_ffn_in = _L0_ffn_setup()
    _d = {'L0_attn_x': _L0_attn_in['x'], 'L0_attn_w_qkv': _L0_attn_in['w_qkv'], 'L0_attn_w_o': _L0_attn_in['w_o'], 'L0_ffn_w1': _L0_ffn_in['w1'], 'L0_ffn_b1': _L0_ffn_in['b1'], 'L0_ffn_w2': _L0_ffn_in['w2'], 'L0_ffn_b2': _L0_ffn_in['b2']}
    _x0 = _d['L0_attn_x']
    _d['L0_attn_x'] = jax.random.normal(jax.random.fold_in(jax.random.key(seed), 1), (1, 2048, 256), dtype=_x0.dtype)
    del _x0
    return _d

def reference(L0_attn_x, L0_attn_w_qkv, L0_attn_w_o, L0_ffn_w1, L0_ffn_b1, L0_ffn_w2, L0_ffn_b2):

    def _L0_attn_ref(x, w_qkv, w_o):
        import jax, jax.numpy as jnp
        import numpy as np
        B, S, H_DIM = (2, 256, 256)
        N_HEADS, D_HEAD = (16, 128)
        b, s, _ = x.shape
        qkv = jnp.einsum('bsh,hf->bsf', x, w_qkv)
        qkv = qkv.reshape(b, s, 3, N_HEADS, D_HEAD)
        q, k, v = (qkv[:, :, 0], qkv[:, :, 1], qkv[:, :, 2])
        q = q.transpose(0, 2, 1, 3)
        k = k.transpose(0, 2, 1, 3)
        v = v.transpose(0, 2, 1, 3)
        scores = jnp.einsum('bhqd,bhkd->bhqk', q, k) / jnp.sqrt(jnp.float32(D_HEAD))
        probs = jax.nn.softmax(scores, axis=-1)
        values = jnp.einsum('bhqk,bhkd->bhkd', probs, v)
        values = values.transpose(0, 2, 1, 3).reshape(b, s, N_HEADS * D_HEAD)
        out = jnp.einsum('bsf,fh->bsh', values, w_o)
        return out

    def _L0_ffn_ref(x, w1, b1, w2, b2):
        import jax, jax.numpy as jnp
        import numpy as np
        EPS = 1e-08

        def _bit_quant(w):
            scale = jnp.maximum(jnp.mean(jnp.abs(w)), EPS)
            w_ternary = jnp.clip(jnp.round(w / scale), -1.0, 1.0)
            return w + jax.lax.stop_gradient(w_ternary - w)
        w1q = _bit_quant(w1)
        w2q = _bit_quant(w2)
        h = jnp.einsum('bsd,fd->bsf', x, w1q) + b1
        h = jax.nn.gelu(h, approximate=False)
        return jnp.einsum('bsf,df->bsd', h, w2q) + b2
    x = L0_attn_x
    x = x + _layernorm(_L0_attn_ref(_layernorm(x, axis=-1), L0_attn_w_qkv, L0_attn_w_o), axis=-1)
    x = x + _layernorm(_L0_ffn_ref(_layernorm(x, axis=-1), L0_ffn_w1, L0_ffn_b1, L0_ffn_w2, L0_ffn_b2), axis=-1)
    return x

_drawn_inputs = setup_inputs


def setup_inputs(seed=0):
    import zlib

    import numpy as np

    out = dict(_drawn_inputs(seed))
    spreads = {}
    factors = {'L0_ffn_b1': 64.0, 'L0_ffn_b2': 64.0}
    for name, (base, spread) in spreads.items():
        noise = np.random.default_rng([zlib.crc32(name.encode()), seed]).standard_normal(out[name].shape)
        drawn = base * np.exp(spread * noise) if base else spread * noise
        out[name] = jnp.asarray(drawn.astype(out[name].dtype))
    for name, factor in factors.items():
        out[name] = (out[name] * factor).astype(out[name].dtype)
    return out
```

```python
from contextlib import ExitStack

import concourse.bass as bass
from concourse import mybir

F32 = mybir.dt.float32
F32R = mybir.dt.float32r
ALU = mybir.AluOpType
ACT = mybir.ActivationFunctionType
AX_X = mybir.AxisListType.X

P = 128
BANK = 512
LN_EPS = 1e-5
QUANT_EPS = 1e-8


def need(eng, sem, count):
    if isinstance(count, int) and count <= 0:
        return
    eng.wait_ge(sem, count)


def sandwich_block(nc, x_in, wqk_in, wv_in, wo_in, w1_in, b1_in, w2_in, b2_in, out):
    TOKENS, HID = x_in.shape
    HEADS, _, HC, D = wv_in.shape
    DFF = w1_in.shape[2]
    TILES = TOKENS // P
    UNITS = TILES
    BANKS = TOKENS // BANK
    FT = DFF // P
    LAST = HEADS - 1
    SCALE = float(D) ** -0.5
    assert D == P and HID == HC * P and UNITS == 4 * BANKS and BANKS == 4 and HEADS % 2 == 0

    YS = TILES // 2
    XB = 4
    BT = TILES // XB
    FFN_PIECES = HC * DFF // BANK
    CHUNK = 2 * P
    CHUNKS = TOKENS // CHUNK

    with ExitStack() as ctx:
        def sb(name, shape, dt=F32):
            return ctx.enter_context(nc.sbuf_tensor(name, shape, dt))

        def sem(name):
            return ctx.enter_context(nc.semaphore(name))

        xt_hi = sb("xt_hi", [P, HC, TOKENS], F32R)
        xt_lo = sb("xt_lo", [P, HC, TOKENS], F32R)
        k_hi = sb("k_hi", [P, 2, TOKENS], F32R)
        k_lo = sb("k_lo", [P, 2, TOKENS], F32R)
        q_hi = sb("q_hi", [P, 2, BANK], F32R)
        q_lo = sb("q_lo", [P, 2, BANK], F32R)
        v_hi = sb("v_hi", [P, 2, BANK], F32R)
        v_lo = sb("v_lo", [P, 2, BANK], F32R)
        probs = sb("probs", [P, 2, TOKENS])
        acc = sb("acc", [P, TILES, HID])
        wqk_hi = sb("wqk_hi", [P, 2, HC, 2 * D], F32R)
        wqk_lo = sb("wqk_lo", [P, 2, HC, 2 * D], F32R)
        wqk_raw = sb("wqk_raw", [P, HC, 2 * D])
        wv_hi = sb("wv_hi", [P, 2, HC, D], F32R)
        wv_lo = sb("wv_lo", [P, 2, HC, D], F32R)
        wv_raw = sb("wv_raw", [P, HC, D])
        wo_hi = sb("wo_hi", [P, 2, HID], F32R)
        wo_lo = sb("wo_lo", [P, 2, HID], F32R)
        wo_raw = sb("wo_raw", [P, HID])
        w2_hi = sb("w2_hi", [P, FT, HID], F32R)
        w2_lo = sb("w2_lo", [P, FT, HID], F32R)
        hid_hi = sb("hid_hi", [P, 2, FT, CHUNK], F32R)
        hid_lo = sb("hid_lo", [P, 2, FT, CHUNK], F32R)
        c_row = sb("c_row", [P, BANK])
        c_col = sb("c_col", [P, BANKS, BANKS])
        tmp = sb("tmp", [P, 2, BANK])
        ffn_raw = sb("ffn_raw", [P, 2, BANK])
        x_stage = sb("x_stage", [P, BT, HID])
        ident = sb("ident", [P, P])
        ones = sb("ones", [P, P])
        b1 = sb("b1", [P, FT])
        b2 = sb("b2", [P, HID])
        qmax = sb("qmax", [P, 2, BANKS])
        negmax = sb("negmax", [P, 2])
        rowsum = sb("rowsum", [P, 2, BANKS])
        total = sb("total", [P, 2])
        rinv = sb("rinv", [P, 2])
        stats = sb("stats", [P, BT, 6])
        mv = sb("mv", [P, TILES, 2])
        var_eps = sb("var_eps", [P, TILES])
        rstd = sb("rstd", [P, TILES])
        neg_half = sb("neg_half", [P, BT])
        abs_piece = sb("abs_piece", [P, 2 * FFN_PIECES])
        scale = sb("scale", [P, 2])
        abs_sum = sb("abs_sum", [P, 2])
        half_scale = sb("half_scale", [P, 2])
        neg_half_scale = sb("neg_half_scale", [P, 2])
        xn = probs[:, :, :].rearrange("p a (t d) -> p (a t) d", d=HID)
        w1_hi = k_hi[:, 0, :].rearrange("p (c f) -> p c f", c=HC)
        w1_lo = k_lo[:, 0, :].rearrange("p (c f) -> p c f", c=HC)
        hidden = probs

        ps_s = ctx.enter_context(nc.psum_tensor("ps_s", [P, BANKS, BANK], F32))
        ps_c = ctx.enter_context(nc.psum_tensor("ps_c", [P, BANK], F32))
        ps_x = ctx.enter_context(nc.psum_tensor("ps_x", [P, 3, BANK], F32))
        X_VALUES, X_QUERIES, X_KEYS = 0, 1, 2
        ps_f = [ps_x[:, X_KEYS, :], ps_c[:, :]]

        x_loaded = [sem(f"x_loaded{b}") for b in range(XB)]
        consts_loaded = sem("consts_loaded")
        wqk_loaded = sem("wqk_loaded")
        wv_loaded = sem("wv_loaded")
        wo_loaded = sem("wo_loaded")
        const_made = sem("const_made")
        ln_var = sem("ln_var")
        ln_rstd = sem("ln_rstd")
        ln_step = sem("ln_step")
        xn_ready = sem("xn_ready")
        xt_ready = sem("xt_ready")
        xt_hi_done = sem("xt_hi_done")
        xt_lo_done = sem("xt_lo_done")
        abs_done = sem("abs_done")
        scale_ready = sem("scale_ready")
        acc_zeroed = sem("acc_zeroed")
        thresholds = sem("thresholds")
        wqk_hi_done = sem("wqk_hi_done")
        wqk_split = sem("wqk_split")
        wv_hi_done = sem("wv_hi_done")
        wv_split = sem("wv_split")
        wo_hi_done = sem("wo_hi_done")
        wo_split = sem("wo_split")
        c_cleared = sem("c_cleared")
        s_ready = sem("s_ready")
        qmax_done = sem("qmax_done")
        max_ready = sem("max_ready")
        exp_done = sem("exp_done")
        rinv_ready = sem("rinv_ready")
        c_added = sem("c_added")
        c_row_done = sem("c_row_done")
        c_turned = sem("c_turned")
        c_col_done = sem("c_col_done")
        k_ready = sem("k_ready")
        k_hi_done = sem("k_hi_done")
        k_lo_done = sem("k_lo_done")
        q_ready = sem("q_ready")
        q_hi_done = sem("q_hi_done")
        q_lo_done = sem("q_lo_done")
        v_ready = sem("v_ready")
        v_hi_done = sem("v_hi_done")
        v_lo_done = sem("v_lo_done")
        y_ready = sem("y_ready")
        y_used = sem("y_used")
        sum_step = sem("sum_step")
        piece_loaded = [sem(f"piece_loaded{i}") for i in range(2)]
        quant_step = sem("quant_step")
        piece_done = sem("piece_done")
        x_again = sem("x_again")
        tr_ready = sem("tr_ready")
        tr_hi_done = sem("tr_hi_done")
        tr_lo_done = sem("tr_lo_done")
        h_ready = sem("h_ready")
        gelu_done = sem("gelu_done")
        h_hi_done = sem("h_hi_done")
        h_lo_done = sem("h_lo_done")
        f_ready = sem("f_ready")
        f_used = sem("f_used")
        local_step = sem("local_step")
        rows_done = sem("rows_done")
        y_stored = sem("y_stored")

        x_tiles = x_in.rearrange("(b t p) d -> b p t d", b=XB, p=P)
        out_tiles = out.rearrange("(c t p) d -> c p t d", t=2, p=P)
        w1_pieces = w1_in.rearrange("p c (s n) -> (c s) p n", n=BANK)
        w2_pieces = w2_in.rearrange("p (s f) d -> s p (f d)", f=BANK // HID)


        block = ctx.enter_context(nc.Block())

        @block.sync
        def _(sp):
            for b in range(XB):
                sp.dma_start(acc[:, b * BT:(b + 1) * BT, :], x_tiles[b]).then_inc(x_loaded[b], 16)
            sp.dma_start(wqk_raw[:, :, :], wqk_in[0]).then_inc(wqk_loaded, 16)
            sp.dma_start(wv_raw[:, :, :], wv_in[0]).then_inc(wv_loaded, 16)
            sp.dma_start(wo_raw[:, :], wo_in[0]).then_inc(wo_loaded, 16)
            sp.dma_start(b1[:, :], b1_in).then_inc(consts_loaded, 16)
            sp.dma_start(b2[:, :], b2_in.partition_broadcast(P)).then_inc(consts_loaded, 16)

            def head_of(w, h):
                if isinstance(h, int):
                    return w[h]
                return w[bass.ds(h, 1)].squeeze(0)

            def query_key_weights(h):
                need(sp, wqk_split, h)
                sp.dma_start(wqk_raw[:, :, :], head_of(wqk_in, h)).then_inc(wqk_loaded, 16)

            def value_output_weights(h):
                need(sp, wv_split, h)
                sp.dma_start(wv_raw[:, :, :], head_of(wv_in, h)).then_inc(wv_loaded, 16)
                need(sp, wo_split, h)
                sp.dma_start(wo_raw[:, :], head_of(wo_in, h)).then_inc(wo_loaded, 16)

            query_key_weights(1)
            for i in range(2 * FFN_PIECES):
                need(sp, abs_done, i - 1)
                src = w1_pieces[i] if i < FFN_PIECES else w2_pieces[i - FFN_PIECES]
                sp.dma_start(ffn_raw[:, i % 2, :], src).then_inc(piece_loaded[i % 2], 16)

            with sp.Fori(2, HEADS) as h:
                query_key_weights(h)
                value_output_weights(h - 1)
            value_output_weights(LAST)
            sp.wait_ge(abs_done, 2 * FFN_PIECES)
            for i in range(2 * FFN_PIECES):
                need(sp, piece_done, i - 1)
                src = w1_pieces[i] if i < FFN_PIECES else w2_pieces[i - FFN_PIECES]
                sp.dma_start(ffn_raw[:, i % 2, :], src).then_inc(piece_loaded[i % 2], 16)
            for b in range(XB):
                need(sp, tr_ready, 2 * b)
                sp.dma_start(x_stage[:, :, :], x_tiles[b]).then_inc(x_again, 16)
            for c in range(CHUNKS):
                sp.wait_ge(rows_done, c + 1)
                sp.dma_start(out_tiles[c], acc[:, 2 * c:2 * c + 2, :]).then_inc(y_stored, 16)
            sp.wait_ge(y_stored, 16 * CHUNKS)

        @block.gpsimd
        def _(pool):
            pool.memset(neg_half[:, :], -0.5).then_inc(const_made, 1)
            pool.memset(ones[:, :], 1.0).then_inc(const_made, 1)
            pool.memset(ident[:, :], 0.0).then_inc(const_made, 1)
            pool.wait_ge(const_made, 3)
            pool.affine_select(out=ident[:, :], in_=ident[:, :], compare_op=ALU.not_equal, fill=1.0, base=0,
                               pattern=[[-1, P]], channel_multiplier=1).then_inc(const_made, 1)

            def inverse_deviation(k, tiles):
                pool.wait_ge(ln_var, k + 1)
                n = tiles.stop - tiles.start
                pool.tensor_tensor(rstd[:, tiles], var_eps[:, tiles], neg_half[:, 0:n], ALU.pow).then_inc(ln_rstd, 1)

            def split(h, raw, hi, lo, loaded, hi_done, done):
                unit = ones[:, 0:1] if len(raw.shape) == 2 else ones[:, 0:1].unsqueeze(2)
                pool.wait_ge(loaded, 16 * (h + 1))
                pool.tensor_tensor(hi, raw, unit.broadcast_to(list(raw.shape)), ALU.mult).then_inc(hi_done, 1)
                pool.wait_ge(hi_done, h + 1)
                pool.tensor_tensor(lo, raw, hi.bitcast(F32), ALU.subtract).then_inc(done, 1)

            def split_query_key(h, par):
                split(h, wqk_raw[:, :, :], wqk_hi[:, par, :, :], wqk_lo[:, par, :, :], wqk_loaded, wqk_hi_done, wqk_split)

            def split_value_output(h, par):
                split(h, wv_raw[:, :, :], wv_hi[:, par, :, :], wv_lo[:, par, :, :], wv_loaded, wv_hi_done, wv_split)
                split(h, wo_raw[:, :], wo_hi[:, par, :], wo_lo[:, par, :], wo_loaded, wo_hi_done, wo_split)

            for b in range(XB):
                inverse_deviation(b, slice(b * BT, (b + 1) * BT))
            split_query_key(0, 0)
            pool.wait_ge(xn_ready, XB)
            pool.memset(acc[:, :, :], 0.0).then_inc(acc_zeroed, 1)
            split_query_key(1, 1)
            split_value_output(0, 0)
            with pool.Fori(0, HEADS // 2 - 1) as it:
                for par in range(2):
                    h = 2 * it + (2 + par)
                    pool.wait_ge(q_ready, 8 * it + (4 * par + 4))
                    split_query_key(h, par)
                    pool.wait_ge(c_added, UNITS * (2 * it + (1 + par)))
                    split_value_output(h - 1, 1 - par)
            pool.wait_ge(c_added, UNITS * LAST)
            split_value_output(LAST, LAST % 2)

            pool.wait_ge(thresholds, 3)
            pool.wait_ge(s_ready, BANKS * UNITS * LAST)
            steps = 0
            for i in range(2 * FFN_PIECES):
                m = i // FFN_PIECES
                part = slice((i % FFN_PIECES) * BANK, (i % FFN_PIECES + 1) * BANK)
                hi = (k_hi[:, 0, :], w2_hi[:, :, :].rearrange("p f d -> p (f d)"))[m][:, part]
                lo = (k_lo[:, 0, :], w2_lo[:, :, :].rearrange("p f d -> p (f d)"))[m][:, part]
                raw = ffn_raw[:, i % 2, :]
                pool.wait_ge(piece_loaded[i % 2], 16 * (FFN_PIECES + i // 2 + 1))

                def then(ins):
                    nonlocal steps
                    steps += 1
                    ins.then_inc(quant_step, 1)
                    pool.wait_ge(quant_step, steps)

                then(pool.tensor_scalar(tmp[:, 0, :], raw, half_scale[:, m:m + 1], None, ALU.is_gt))
                then(pool.tensor_scalar(tmp[:, 1, :], raw, neg_half_scale[:, m:m + 1], None, ALU.is_lt))
                then(pool.tensor_tensor(tmp[:, 0, :], tmp[:, 0, :], tmp[:, 1, :], ALU.subtract))
                then(pool.tensor_tensor(tmp[:, 0, :], tmp[:, 0, :], raw, ALU.subtract))
                then(pool.tensor_tensor(tmp[:, 1, :], tmp[:, 0, :], raw, ALU.add))
                then(pool.tensor_copy(hi, tmp[:, 1, :]))
                pool.tensor_tensor(lo, tmp[:, 1, :], hi.bitcast(F32), ALU.subtract).then_inc(piece_done, 1)
                pool.wait_ge(piece_done, i + 1)
            sets = XB

            def both_norms(b):
                nonlocal sets
                for _ in range(2):
                    inverse_deviation(sets, slice(b * BT, (b + 1) * BT))
                    sets += 1

            both_norms(0)
            for c in range(CHUNKS + 1):
                if c:
                    inverse_deviation(sets, slice(2 * c - 2, 2 * c))
                    sets += 1
                if c % 2 == 0 and c // 2 + 1 < XB:
                    both_norms(c // 2 + 1)

        @block.tensor
        def _(pe):
            def product(ps, pairs, first=True, last=True):
                n = 3 * len(pairs)
                i = 0
                for ah, al, bh, bl in pairs:
                    for a, b in ((ah, bh), (ah, bl), (al, bh)):
                        ins = pe.matmul(ps, a, b, start=first and i == 0, stop=last and i == n - 1)
                        i += 1
                return ins

            def project(ps, w_h, w_l, cols, chunk):
                toks = slice(chunk * BANK, (chunk + 1) * BANK)
                return product(ps, [(w_h[:, c, cols], w_l[:, c, cols], xt_hi[:, c, toks], xt_lo[:, c, toks])
                                    for c in range(HC)])

            def queries(ps, par, chunk):
                return project(ps, wqk_hi[:, par], wqk_lo[:, par], slice(0, D), chunk)

            def keys(ps, par, chunk):
                return project(ps, wqk_hi[:, par], wqk_lo[:, par], slice(D, 2 * D), chunk)

            pe.wait_ge(const_made, 4)
            for g in range(TILES // 2):
                pe.wait_ge(xn_ready, g // 2 + 1)
                need(pe, xt_lo_done, g - 3)
                for c in range(HC):
                    for t in range(2):
                        ins = pe.transpose(ps_s[:, g % 4, (2 * c + t) * P:(2 * c + t + 1) * P],
                                           xn[:, 2 * g + t, c * P:(c + 1) * P], ident[:, :])
                ins.then_inc(xt_ready, 1)
            pe.wait_ge(wqk_split, 1)
            for c in range(BANKS):
                pe.wait_ge(xt_lo_done, max(2 * c + 2, 4 + c + 1))
                keys(ps_s[:, c, :], 0, c).then_inc(k_ready, 1)
                if c == 0:
                    queries(ps_x[:, X_QUERIES, :], 0, 0).then_inc(q_ready, 1)

            def scores(h, par, r, bank):
                n = UNITS * h + r
                need(pe, exp_done, BANKS * (n - 1) + bank + 1)
                if bank == 0 and r % 4 == 0:
                    pe.wait_ge(q_lo_done, 4 * h + r // 4 + 1)
                if r == 0:
                    pe.wait_ge(k_lo_done, 4 * h + bank + 1)
                qs = slice((r % 4) * P, (r % 4 + 1) * P)
                ks = slice(bank * BANK, (bank + 1) * BANK)
                q = (r // 4) % 2
                product(ps_s[:, bank, :], [(q_hi[:, q, qs], q_lo[:, q, qs], k_hi[:, par, ks], k_lo[:, par, ks])])\
                    .then_inc(s_ready, 1)

            def sums_over_queries(n, u):
                pe.wait_ge(rinv_ready, n + 1)
                for b in range(BANKS):
                    ins = pe.matmul(ps_c[32 * b:32 * b + 1, :], rinv[:, u % 2:u % 2 + 1],
                                    probs[:, u % 2, b * BANK:(b + 1) * BANK], start=u == 0, stop=u == UNITS - 1)
                ins.then_inc(c_added, 1)

            def output(y, par):
                vb, x = (y // 2) % 2, y % 2
                for s in range(2):
                    ts = slice((y % 2) * CHUNK + s * P, (y % 2) * CHUNK + (s + 1) * P)
                    ins = product(ps_x[:, x, s * HID:(s + 1) * HID],
                                  [(v_hi[:, vb, ts], v_lo[:, vb, ts], wo_hi[:, par, :], wo_lo[:, par, :])])
                ins.then_inc(y_ready, 1)

            def slot(h, par, r, h0=False, last=False, after=False):
                n, c = UNITS * h + r, r // 4
                if not after:
                    for bank in range(BANKS):
                        scores(h, par, r, bank)
                if r == 0 and not h0 or r > 0 and not after:
                    if r == 1 and not h0:
                        pe.wait_ge(c_row_done, h)
                    if h0 and r == 1:
                        pe.wait_ge(c_cleared, 1)
                    sums_over_queries(n - 1, (r - 1) % UNITS)
                if r % 4 == 0 and not last and not after:
                    need(pe, k_lo_done, 4 * (h + 1) + c)
                    if r == 0:
                        pe.wait_ge(wqk_split, h + 2)
                    if r == 4 and not h0:
                        pe.wait_ge(c_col_done, h)
                    keys(ps_x[:, X_KEYS, :], 1 - par, c).then_inc(k_ready, 1)
                if r % 4 == 1 and not h0:
                    need(pe, y_used, YS * (h - 1) + 2 * c - 1)
                    if r == 1:
                        pe.wait_ge(wv_split, h)
                    project(ps_x[:, X_VALUES, :], wv_hi[:, 1 - par], wv_lo[:, 1 - par], slice(0, D), c).then_inc(v_ready, 1)
                if r % 4 == 2 and not after and not (last and c == 3):
                    need(pe, y_used, YS * (h - 1) + 2 * c)
                    queries(ps_x[:, X_QUERIES, :], par if c < 3 else 1 - par, (c + 1) % 4).then_inc(q_ready, 1)
                if r == 2 and not h0:
                    pe.wait_ge(c_row_done, h)
                    pe.wait_ge(k_lo_done, 4 * HEADS if last or after else 4 * (h + 1) + 1)
                    for s in range(BANKS):
                        ins = pe.matmul(ps_x[:, X_KEYS, 4 * s:4 * s + 4], c_row[:, s * P:(s + 1) * P],
                                        ident[:, 0:P:32], start=True, stop=True)
                    ins.then_inc(c_turned, 1)
                if r % 4 == 3 and not h0:
                    pe.wait_ge(v_lo_done, 4 * (h - 1) + c + 1)
                    if r == 3:
                        pe.wait_ge(wo_split, h)
                    output(2 * c, 1 - par)
                    if after or last and c == 3:
                        pe.wait_ge(y_used, YS * (h - 1) + 2 * c)
                    else:
                        pe.wait_ge(q_lo_done, 4 * h + c + 2)
                    output(2 * c + 1, 1 - par)
                if h0 and r == 12:
                    pe.wait_ge(abs_done, 2 * FFN_PIECES + 2)
                    pe.matmul(ps_x[:, X_VALUES, 0:2], ones[:, :], abs_sum[:, :], start=True, stop=True)\
                        .then_inc(scale_ready, 1)
                if h0 and r == 15:
                    pe.wait_ge(thresholds, 1)

            def head(h, par, h0=False, last=False, after=False):
                for r in range(UNITS):
                    slot(h, par, r, h0, last, after)

            head(0, 0, h0=True)
            head(1, 1)
            with pe.Fori(1, HEADS // 2 - 1) as it:
                head(2 * it, 0)
                head(2 * it + 1, 1)
            head(LAST - 1, 0)
            head(LAST, 1, last=True)
            head(HEADS, 0, after=True)

            pe.wait_ge(piece_done, 2 * FFN_PIECES)

            def turn_block_input(b):
                pe.wait_ge(xn_ready, XB + b + 1)
                for g in range(2 * b, 2 * b + 2):
                    need(pe, tr_lo_done, g - 1)
                    for c in range(HC):
                        for t in range(2):
                            ins = pe.transpose(ps_x[:, g % 2, (2 * c + t) * P:(2 * c + t + 1) * P],
                                               x_stage[:, (2 * g + t) % BT, c * P:(c + 1) * P], ident[:, :])
                    ins.then_inc(tr_ready, 1)

            def up(c):
                pe.wait_ge(tr_lo_done, c + 1)
                toks = slice(c * CHUNK, (c + 1) * CHUNK)
                for f in range(FT):
                    if f % 2 == 0:
                        need(pe, gelu_done, FT * (c - 1) + f + 2)
                    fs = slice(f * P, (f + 1) * P)
                    product(ps_s[:, f // 2, (f % 2) * CHUNK:(f % 2 + 1) * CHUNK],
                            [(w1_hi[:, k, fs], w1_lo[:, k, fs], xt_hi[:, k, toks], xt_lo[:, k, toks]) for k in range(HC)])\
                        .then_inc(h_ready, 1)

            def down(c):
                pe.wait_ge(h_lo_done, c + 1)
                need(pe, f_used, c - 1)
                for t in range(2):
                    ts = slice(t * P, (t + 1) * P)
                    ins = product(ps_f[c % 2][:, t * HID:(t + 1) * HID],
                                  [(hid_hi[:, c % 2, f, ts], hid_lo[:, c % 2, f, ts], w2_hi[:, f, :], w2_lo[:, f, :])
                                   for f in range(FT)])
                ins.then_inc(f_ready, 1)

            pe.wait_ge(y_used, YS * HEADS)
            turn_block_input(0)
            for c in range(CHUNKS):
                up(c)
                if c:
                    down(c - 1)
                if c % 2 and (c + 1) // 2 < XB:
                    turn_block_input((c + 1) // 2)
            down(CHUNKS - 1)

        @block.scalar
        def _(act):
            for g in range(TILES // 2):
                act.wait_ge(xt_ready, g + 1)
                act.activation(xt_hi[:, :, g * CHUNK:(g + 1) * CHUNK],
                               ps_s[:, g % 4, :].rearrange("p (c n) -> p c n", c=HC), ACT.Copy).then_inc(xt_hi_done, 1)

            def keys(h, par, c, src):
                act.wait_ge(k_ready, 4 * h + c + 1)
                act.activation(k_hi[:, par, c * BANK:(c + 1) * BANK], src, ACT.Copy).then_inc(k_hi_done, 1)

            def queries(h, c):
                act.wait_ge(q_ready, 4 * h + c + 1)
                act.activation(q_hi[:, c % 2, :], ps_x[:, X_QUERIES, :], ACT.Copy, scale=SCALE).then_inc(q_hi_done, 1)

            for c in range(BANKS):
                keys(0, 0, c, ps_s[:, c, :])
                if c == 0:
                    queries(0, 0)

            def exp_unit(n, r):
                act.wait_ge(max_ready, n + 1)
                for b in range(BANKS):
                    act.activation(probs[:, r % 2, b * BANK:(b + 1) * BANK], ps_s[:, b, :], ACT.Exp,
                                   bias=negmax[:, r % 2:r % 2 + 1], scale=1.0,
                                   accum_out=rowsum[:, r % 2, b:b + 1]).then_inc(exp_done, 1)

            def slot(h, par, r, h0=False, last=False, after=False):
                c = r // 4
                if r == 1 and not h0:
                    act.wait_ge(c_added, UNITS * h)
                    need(act, c_turned, h - 1)
                    act.activation(c_row[:, :], ps_c[:, :], ACT.Copy).then_inc(c_row_done, 1)
                if r % 4 == 1 and not last and not after:
                    keys(h + 1, 1 - par, c, ps_x[:, X_KEYS, :])
                if r % 4 == 2 and not h0:
                    act.wait_ge(v_ready, 4 * (h - 1) + c + 1)
                    if c < 2:
                        need(act, y_ready, YS * (h - 2) + 2 * c + 6)
                    act.activation(v_hi[:, c % 2, :], ps_x[:, X_VALUES, :], ACT.Copy).then_inc(v_hi_done, 1)
                if r % 4 == 3 and not after and not (last and c == 3):
                    queries(h, c + 1)
                if not after:
                    exp_unit(UNITS * h + r, r)

            def head(h, par, h0=False, last=False, after=False):
                for r in range(UNITS):
                    slot(h, par, r, h0, last, after)

            head(0, 0, h0=True)
            head(1, 1)
            with act.Fori(1, HEADS // 2 - 1) as it:
                head(2 * it, 0)
                head(2 * it + 1, 1)
            head(LAST - 1, 0)
            head(LAST, 1, last=True)
            head(HEADS, 0, after=True)

            act.wait_ge(consts_loaded, 32)

            def split_turned(g):
                act.wait_ge(tr_ready, g + 1)
                act.activation(xt_hi[:, :, g * CHUNK:(g + 1) * CHUNK],
                               ps_x[:, g % 2, :].rearrange("p (c n) -> p c n", c=HC), ACT.Copy).then_inc(tr_hi_done, 1)

            split_turned(0)
            split_turned(1)
            for c in range(CHUNKS):
                need(act, h_lo_done, c - 1)
                for f in range(FT):
                    if f % 2 == 0:
                        act.wait_ge(h_ready, FT * c + f + 2)
                    act.activation(hidden[:, c % 2, f * CHUNK:(f + 1) * CHUNK],
                                   ps_s[:, f // 2, (f % 2) * CHUNK:(f % 2 + 1) * CHUNK], ACT.Gelu,
                                   bias=b1[:, f:f + 1], scale=1.0).then_inc(gelu_done, 1)
                if c % 2 and (c + 1) // 2 < XB:
                    split_turned(c + 1)
                    split_turned(c + 2)

        @block.vector
        def _(dve):
            ln_steps = 0

            def variances(sets, tiles, src, wait_src=None):
                nonlocal ln_steps
                for i, t in enumerate(tiles):
                    dve.bn_stats(stats[:, i, :], src(t)).then_inc(ln_step, 1)
                    ln_steps += 1
                first = ln_steps - len(tiles)
                for i, t in enumerate(tiles):
                    dve.wait_ge(ln_step, first + i + 1)
                    dve.bn_aggr(mv[:, t, :], stats[:, i, :]).then_inc(ln_step, 1)
                    ln_steps += 1
                dve.wait_ge(ln_step, ln_steps)
                a, b = tiles[0], tiles[-1] + 1
                dve.tensor_scalar(var_eps[:, a:b], mv[:, a:b, 1], LN_EPS, None, ALU.add).then_inc(ln_var, 1)

            def normalise(dst, src, t):
                return dve.tensor_scalar(dst, src, mv[:, t, 0:1], rstd[:, t:t + 1], ALU.subtract, ALU.mult)

            batch = [list(range(b * BT, (b + 1) * BT)) for b in range(XB)]

            def normalise_input(b):
                dve.wait_ge(ln_rstd, b + 1)
                for t in batch[b]:
                    ins = normalise(xn[:, t, :], acc[:, t, :], t)
                ins.then_inc(xn_ready, 1)

            for b in range(XB):
                dve.wait_ge(x_loaded[b], 16)
                if b:
                    dve.wait_ge(ln_step, ln_steps)
                variances(b, batch[b], lambda t: acc[:, t, :])
                if b:
                    normalise_input(b - 1)
            normalise_input(XB - 1)

            for g in range(TILES // 2):
                dve.wait_ge(xt_hi_done, g + 1)
                hi = xt_hi[:, :, g * CHUNK:(g + 1) * CHUNK]
                dve.tensor_tensor(xt_lo[:, :, g * CHUNK:(g + 1) * CHUNK],
                                  ps_s[:, g % 4, :].rearrange("p (c n) -> p c n", c=HC), hi.bitcast(F32),
                                  ALU.subtract).then_inc(xt_lo_done, 1)

            dve.memset(ps_c[:, :], 0.0).then_inc(c_cleared, 1)

            def keys(h, par, c, src):
                dve.wait_ge(k_hi_done, 4 * h + c + 1)
                ks = slice(c * BANK, (c + 1) * BANK)
                dve.tensor_tensor(k_lo[:, par, ks], src, k_hi[:, par, ks].bitcast(F32), ALU.subtract).then_inc(k_lo_done, 1)

            def queries(h, c):
                dve.wait_ge(q_hi_done, 4 * h + c + 1)
                dve.scalar_tensor_tensor(out=q_lo[:, c % 2, :], in0=ps_x[:, X_QUERIES, :], scalar=SCALE,
                                         in1=q_hi[:, c % 2, :].bitcast(F32), op0=ALU.mult, op1=ALU.subtract)\
                    .then_inc(q_lo_done, 1)

            for c in range(BANKS):
                keys(0, 0, c, ps_s[:, c, :])
                if c == 0:
                    queries(0, 0)

            def sum_magnitudes(i):
                dve.wait_ge(piece_loaded[i % 2], 16 * (i // 2 + 1))
                dve.tensor_reduce(abs_piece[:, i:i + 1], ffn_raw[:, i % 2, :], AX_X, ALU.add,
                                  apply_absolute_value=True).then_inc(abs_done, 1)

            def sum_pieces():
                dve.wait_ge(abs_done, 2 * FFN_PIECES)
                for m in range(2):
                    dve.tensor_reduce(abs_sum[:, m:m + 1], abs_piece[:, m * FFN_PIECES:(m + 1) * FFN_PIECES], AX_X,
                                      ALU.add).then_inc(abs_done, 1)

            def make_thresholds():
                dve.wait_ge(scale_ready, 1)
                dve.tensor_scalar(scale[:, :], ps_x[:, X_VALUES, 0:2], 1.0 / (HID * DFF), QUANT_EPS, ALU.mult, ALU.max)\
                    .then_inc(thresholds, 1)
                dve.wait_ge(thresholds, 1)
                dve.tensor_scalar(half_scale[:, :], scale[:, :], 0.5, None, ALU.mult).then_inc(thresholds, 1)
                dve.tensor_scalar(neg_half_scale[:, :], scale[:, :], -0.5, None, ALU.mult).then_inc(thresholds, 1)

            def bank_max(n, r, bank):
                dve.wait_ge(s_ready, 4 * n + bank + 1)
                dve.tensor_reduce(qmax[:, r % 2, bank:bank + 1], ps_s[:, bank, :], AX_X, ALU.max).then_inc(qmax_done, 1)

            def row_max(n, r):
                dve.wait_ge(qmax_done, 4 * n + BANKS)
                dve.tensor_reduce(negmax[:, r % 2:r % 2 + 1], qmax[:, r % 2, :], AX_X, ALU.max,
                                  negate=True).then_inc(max_ready, 1)

            def row_sum(n, u):
                dve.wait_ge(exp_done, BANKS * (n + 1))
                dve.tensor_reduce(total[:, u % 2:u % 2 + 1], rowsum[:, u % 2, :], AX_X, ALU.add).then_inc(sum_step, 1)
                dve.wait_ge(sum_step, n + 1)
                dve.reciprocal(rinv[:, u % 2:u % 2 + 1], total[:, u % 2:u % 2 + 1]).then_inc(rinv_ready, 1)

            def add_rows(h, y):
                dve.wait_ge(y_ready, YS * h + y + 1)
                if y == 0:
                    dve.wait_ge(c_col_done, h + 1)
                    dve.wait_ge(acc_zeroed, 1)
                need(dve, y_used, YS * h + y)
                for s in range(2):
                    tile = 2 * y + s
                    a, b = tile % BANKS, tile // BANKS
                    ins = dve.scalar_tensor_tensor(out=acc[:, tile, :], in0=ps_x[:, y % 2, s * HID:(s + 1) * HID],
                                                   scalar=c_col[:, a, b:b + 1], in1=acc[:, tile, :],
                                                   op0=ALU.mult, op1=ALU.add)
                ins.then_inc(y_used, 1)

            def slot(h, par, r, h0=False, last=False, after=False):
                n, c = UNITS * h + r, r // 4
                if not after:
                    bank_max(n, r, 0)
                    bank_max(n, r, 1)
                if r == 0 and not h0 or r > 0 and not after:
                    row_sum(n - 1, (r - 1) % UNITS)
                if not after:
                    bank_max(n, r, 2)
                    bank_max(n, r, 3)
                    row_max(n, r)
                if r % 4 == 0 and not h0 and (r > 0 or not isinstance(h, int) or h > 1):
                    pair(h - 1 if r else h - 2, (2 * c - 2) % YS)
                if r % 4 == 1 and not last and not after:
                    keys(h + 1, 1 - par, c, ps_x[:, X_KEYS, :])
                if r % 4 == 2 and not h0:
                    dve.wait_ge(v_hi_done, 4 * (h - 1) + c + 1)
                    dve.tensor_tensor(v_lo[:, c % 2, :], ps_x[:, X_VALUES, :], v_hi[:, c % 2, :].bitcast(F32),
                                      ALU.subtract).then_inc(v_lo_done, 1)
                if r % 4 == 3 and not after and not (last and c == 3):
                    queries(h, c + 1)
                if r == 3 and not h0:
                    dve.wait_ge(c_turned, h)
                    need(dve, y_used, YS * (h - 1))
                    dve.tensor_copy(c_col[:, :, :], ps_x[:, X_KEYS, 0:16].rearrange("p (a b) -> p a b", a=BANKS))\
                        .then_inc(c_col_done, 1)

            def pair(h, y):
                add_rows(h, y)
                add_rows(h, y + 1)

            def head(h, par, h0=False, last=False, after=False):
                for r in range(UNITS):
                    slot(h, par, r, h0, last, after)
                    if h0 and 2 <= r < 2 + 2 * FFN_PIECES:
                        sum_magnitudes(r - 2)
                    if h0 and r == 2 + 2 * FFN_PIECES:
                        sum_pieces()
                    if h0 and r == 12:
                        make_thresholds()

            head(0, 0, h0=True)
            head(1, 1)
            with dve.Fori(1, HEADS // 2 - 1) as it:
                head(2 * it, 0)
                head(2 * it + 1, 1)
            head(LAST - 1, 0)
            head(LAST, 1, last=True)
            head(HEADS, 0, after=True)
            pair(LAST, YS - 2)

            sets = XB

            def deviations(tiles, src):
                nonlocal sets
                dve.wait_ge(ln_step, ln_steps)
                variances(sets, tiles, src)
                sets += 1
                dve.wait_ge(ln_rstd, sets)

            def then(ins):
                nonlocal local_steps
                local_steps += 1
                ins.then_inc(local_step, 1)

            def settled():
                dve.wait_ge(local_step, local_steps)

            local_steps = 0

            def block_input(b):
                deviations(batch[b], lambda t: acc[:, t, :])
                for t in batch[b]:
                    then(normalise(acc[:, t, :], acc[:, t, :], t))
                dve.wait_ge(x_again, 16 * (b + 1))
                settled()
                for t in batch[b]:
                    then(dve.tensor_tensor(acc[:, t, :], acc[:, t, :], x_stage[:, t % BT, :], ALU.add))
                settled()
                deviations(batch[b], lambda t: acc[:, t, :])
                for t in batch[b]:
                    ins = normalise(x_stage[:, t % BT, :], acc[:, t, :], t)
                ins.then_inc(xn_ready, 1)

            def split_turned(g):
                dve.wait_ge(tr_hi_done, g + 1)
                toks = slice(g * CHUNK, (g + 1) * CHUNK)
                dve.tensor_tensor(xt_lo[:, :, toks], ps_x[:, g % 2, :].rearrange("p (c n) -> p c n", c=HC),
                                  xt_hi[:, :, toks].bitcast(F32), ALU.subtract).then_inc(tr_lo_done, 1)

            def split_hidden(c):
                dve.wait_ge(gelu_done, FT * (c + 1))
                need(dve, f_ready, c - 1)
                hi, lo = hid_hi[:, c % 2, :, :], hid_lo[:, c % 2, :, :]
                h = hidden[:, c % 2, :].rearrange("p (f n) -> p f n", f=FT)
                dve.tensor_copy(hi, h).then_inc(h_hi_done, 1)
                dve.wait_ge(h_hi_done, c + 1)
                dve.tensor_tensor(lo, h, hi.bitcast(F32), ALU.subtract).then_inc(h_lo_done, 1)

            def finish(c):
                dve.wait_ge(f_ready, c + 1)
                need(dve, rows_done, c)
                ffn = tmp[:, 0, :].rearrange("p (t d) -> p t d", t=2)
                for t in range(2):
                    ins = dve.tensor_tensor(ffn[:, t, :], ps_f[c % 2][:, t * HID:(t + 1) * HID], b2[:, :], ALU.add)
                ins.then_inc(f_used, 1)
                dve.wait_ge(f_used, c + 1)
                deviations([2 * c, 2 * c + 1], lambda t: ffn[:, t % 2, :])
                for t in range(2):
                    then(normalise(ffn[:, t, :], ffn[:, t, :], 2 * c + t))
                settled()
                tiles = slice(2 * c, 2 * c + 2)
                dve.tensor_tensor(acc[:, tiles, :], acc[:, tiles, :], ffn, ALU.add).then_inc(rows_done, 1)

            dve.wait_ge(y_used, YS * HEADS)
            dve.wait_ge(consts_loaded, 32)
            block_input(0)
            split_turned(0)
            split_turned(1)
            for c in range(CHUNKS):
                split_hidden(c)
                if c % 2 and (c + 1) // 2 < XB:
                    split_turned(c + 1)
                    split_turned(c + 2)
                if c:
                    finish(c - 1)
                if c % 2 == 0 and c // 2 + 1 < XB:
                    block_input(c // 2 + 1)
            finish(CHUNKS - 1)


def kernel(L0_attn_x, L0_attn_w_qkv, L0_attn_w_o, L0_ffn_w1, L0_ffn_b1, L0_ffn_w2, L0_ffn_b2):
    import numpy as np
    import concourse.bacc as bacc
    from concourse.bass_utils import run_bass_kernel_spmd

    x = np.asarray(L0_attn_x)
    batch, tokens, hid = x.shape
    d = P
    heads = L0_attn_w_o.shape[0] // d
    dff = L0_ffn_w1.shape[0]
    hc = hid // P
    w_qkv = np.asarray(L0_attn_w_qkv).reshape(hc, P, 3, heads, d)
    arrays = {
        "x": x.reshape(batch * tokens, hid),
        "w_qk": w_qkv[:, :, 0:2].transpose(3, 1, 0, 2, 4).reshape(heads, P, hc, 2 * d),
        "w_v": w_qkv[:, :, 2].transpose(2, 1, 0, 3),
        "w_o": np.asarray(L0_attn_w_o).reshape(heads, d, hid),
        "w1": np.asarray(L0_ffn_w1).T.reshape(hc, P, dff).transpose(1, 0, 2),
        "b1": np.asarray(L0_ffn_b1).reshape(dff // P, P).T,
        "w2": np.asarray(L0_ffn_w2).T.reshape(dff // P, P, hid).transpose(1, 0, 2),
        "b2": np.asarray(L0_ffn_b2),
    }
    arrays = {f"in_{k}": np.ascontiguousarray(v) for k, v in arrays.items()}
    nc = bacc.Bacc("TRN2", target_bir_lowering=False, num_devices=1)
    ins = [nc.dram_tensor(k, v.shape, mybir.dt.from_np(v.dtype), kind="ExternalInput").ap() for k, v in arrays.items()]
    out = nc.dram_tensor("out", (batch * tokens, hid), F32, kind="ExternalOutput").ap()
    sandwich_block(nc, *ins, out)
    result = run_bass_kernel_spmd(nc, [arrays], core_ids=[0])
    return result.results[0]["out"].reshape(batch, tokens, hid)
```

```python
from contextlib import ExitStack

import concourse.bass as bass
from concourse import mybir

F32 = mybir.dt.float32
F32R = mybir.dt.float32r
ALU = mybir.AluOpType
ACT = mybir.ActivationFunctionType
AX_X = mybir.AxisListType.X

P = 128
BANK = 512
LN_EPS = 1e-5
QUANT_EPS = 1e-8


def need(eng, sem, count):
    if isinstance(count, int) and count <= 0:
        return
    eng.wait_ge(sem, count)


def sandwich_block(nc, x_in, wqk_in, wv_in, wo_in, w1_in, b1_in, w2_in, b2_in, out):
    TOKENS, HID = x_in.shape
    HEADS, _, HC, D = wv_in.shape
    DFF = w1_in.shape[2]
    TILES = TOKENS // P
    UNITS = TILES
    BANKS = TOKENS // BANK
    FT = DFF // P
    LAST = HEADS - 1
    SCALE = float(D) ** -0.5
    assert D == P and HID == HC * P and UNITS == 4 * BANKS and BANKS == 4 and HEADS % 2 == 0

    YS = TILES // 2
    XB = 4
    BT = TILES // XB
    FFN_PIECES = HC * DFF // BANK
    CHUNK = 2 * P
    CHUNKS = TOKENS // CHUNK
    BY_POOL = list(range(0, UNITS - 3, 2))
    ADDS = len(BY_POOL) - 1
    PE_SUMS = UNITS - len(BY_POOL) + 1

    with ExitStack() as ctx:
        def sb(name, shape, dt=F32):
            return ctx.enter_context(nc.sbuf_tensor(name, shape, dt))

        def sem(name):
            return ctx.enter_context(nc.semaphore(name))

        xt_hi = sb("xt_hi", [P, HC, TOKENS], F32R)
        xt_lo = sb("xt_lo", [P, HC, TOKENS], F32R)
        k_hi = sb("k_hi", [P, 2, TOKENS], F32R)
        k_lo = sb("k_lo", [P, 2, TOKENS], F32R)
        q_hi = sb("q_hi", [P, 2, BANK], F32R)
        q_lo = sb("q_lo", [P, 2, BANK], F32R)
        v_hi = sb("v_hi", [P, 2, BANK], F32R)
        v_lo = sb("v_lo", [P, 2, BANK], F32R)
        probs = sb("probs", [P, 2, TOKENS])
        acc = sb("acc", [P, TILES, HID])
        wqk_hi = sb("wqk_hi", [P, 2, HC, 2 * D], F32R)
        wqk_lo = sb("wqk_lo", [P, 2, HC, 2 * D], F32R)
        wqk_raw = sb("wqk_raw", [P, HC, 2 * D])
        wv_hi = sb("wv_hi", [P, 2, HC, D], F32R)
        wv_lo = sb("wv_lo", [P, 2, HC, D], F32R)
        wv_raw = sb("wv_raw", [P, HC, D])
        wo_hi = sb("wo_hi", [P, 2, HID], F32R)
        wo_lo = sb("wo_lo", [P, 2, HID], F32R)
        wo_raw = sb("wo_raw", [P, HID])
        w2_hi = sb("w2_hi", [P, FT, HID], F32R)
        w2_lo = sb("w2_lo", [P, FT, HID], F32R)
        hid_hi = sb("hid_hi", [P, 2, FT, CHUNK], F32R)
        with nc.sbuf_tensor("weighted_sum", [P, TOKENS], F32) as weighted_sum, \
                nc.sbuf_tensor("weighted", [P, TOKENS], F32) as weighted:
            pass
        hid_lo = sb("hid_lo", [P, 2, FT, CHUNK], F32R)
        c_row = sb("c_row", [P, BANK])
        c_col = sb("c_col", [P, BANKS, BANKS])
        tmp = sb("tmp", [P, 2, BANK])
        ffn_raw = sb("ffn_raw", [P, 2, BANK])
        x_stage = sb("x_stage", [P, 2, BT, HID])
        ident = sb("ident", [P, P])
        ones = sb("ones", [P, P])
        b1 = sb("b1", [P, FT])
        b2 = sb("b2", [P, HID])
        qmax = sb("qmax", [P, 2, BANKS])
        negmax = sb("negmax", [P, 2])
        rowsum = sb("rowsum", [P, 2, BANKS])
        total = sb("total", [P, 2])
        rinv = sb("rinv", [P, 2])
        stats = sb("stats", [P, BT, 6])
        mv = sb("mv", [P, TILES, 2])
        var_eps = sb("var_eps", [P, TILES])
        rstd = sb("rstd", [P, TILES])
        neg_half = sb("neg_half", [P, BT])
        abs_piece = sb("abs_piece", [P, 2 * FFN_PIECES])
        scale = sb("scale", [P, 2])
        abs_sum = sb("abs_sum", [P, 2])
        half_scale = sb("half_scale", [P, 2])
        neg_half_scale = sb("neg_half_scale", [P, 2])
        xn = probs[:, :, :].rearrange("p a (t d) -> p (a t) d", d=HID)
        w1_hi = k_hi[:, 0, :].rearrange("p (c f) -> p c f", c=HC)
        w1_lo = k_lo[:, 0, :].rearrange("p (c f) -> p c f", c=HC)
        hidden = probs

        ps_s = ctx.enter_context(nc.psum_tensor("ps_s", [P, BANKS, BANK], F32))
        ps_c = ctx.enter_context(nc.psum_tensor("ps_c", [P, BANK], F32))
        ps_x = ctx.enter_context(nc.psum_tensor("ps_x", [P, 3, BANK], F32))
        X_VALUES, X_KEYS, X_COLUMNS = 0, 1, 2
        X_QUERIES = X_KEYS
        X_ROWS = (X_VALUES, X_COLUMNS)
        ps_turned = [ps_x[:, X_KEYS, :], ps_c[:, :]]
        ps_f = [ps_x[:, X_COLUMNS, :], ps_x[:, X_VALUES, :]]

        x_loaded = [sem(f"x_loaded{b}") for b in range(XB)]
        consts_loaded = sem("consts_loaded")
        wqk_loaded = sem("wqk_loaded")
        wv_loaded = sem("wv_loaded")
        wo_loaded = sem("wo_loaded")
        const_made = sem("const_made")
        ln_var = sem("ln_var")
        ln_rstd = sem("ln_rstd")
        ln_step = sem("ln_step")
        xn_ready = sem("xn_ready")
        xt_ready = sem("xt_ready")
        xt_hi_done = sem("xt_hi_done")
        xt_lo_done = sem("xt_lo_done")
        abs_done = sem("abs_done")
        scale_ready = sem("scale_ready")
        acc_zeroed = sem("acc_zeroed")
        thresholds = sem("thresholds")
        wqk_hi_done = sem("wqk_hi_done")
        wqk_split = sem("wqk_split")
        wv_hi_done = sem("wv_hi_done")
        wv_split = sem("wv_split")
        wo_hi_done = sem("wo_hi_done")
        wo_split = sem("wo_split")
        c_cleared = sem("c_cleared")
        s_ready = sem("s_ready")
        qmax_done = sem("qmax_done")
        max_ready = sem("max_ready")
        exp_done = sem("exp_done")
        rinv_ready = sem("rinv_ready")
        c_added = sem("c_added")
        weighted_ready = sem("weighted_ready")
        weighted_added = sem("weighted_added")
        c_row_done = sem("c_row_done")
        c_turned = sem("c_turned")
        c_col_done = sem("c_col_done")
        k_ready = sem("k_ready")
        k_hi_done = sem("k_hi_done")
        k_lo_done = sem("k_lo_done")
        q_ready = sem("q_ready")
        q_hi_done = sem("q_hi_done")
        q_lo_done = sem("q_lo_done")
        v_ready = sem("v_ready")
        v_hi_done = sem("v_hi_done")
        v_lo_done = sem("v_lo_done")
        y_ready = sem("y_ready")
        y_used = sem("y_used")
        sum_step = sem("sum_step")
        piece_loaded = [sem(f"piece_loaded{i}") for i in range(2)]
        quant_step = sem("quant_step")
        piece_done = sem("piece_done")
        x_again = [sem(f"x_again{i}") for i in range(2)]
        tr_ready = sem("tr_ready")
        tr_hi_done = sem("tr_hi_done")
        tr_lo_done = sem("tr_lo_done")
        h_ready = sem("h_ready")
        gelu_done = sem("gelu_done")
        h_hi_done = sem("h_hi_done")
        h_lo_done = sem("h_lo_done")
        f_ready = sem("f_ready")
        f_used = sem("f_used")
        local_step = sem("local_step")
        rows_done = sem("rows_done")
        y_stored = sem("y_stored")

        x_tiles = x_in.rearrange("(b t p) d -> b p t d", b=XB, p=P)
        out_tiles = out.rearrange("(c t p) d -> c p t d", t=2, p=P)
        w1_pieces = w1_in.rearrange("p c (s n) -> (c s) p n", n=BANK)
        w2_pieces = w2_in.rearrange("p (s f) d -> s p (f d)", f=BANK // HID)


        block = ctx.enter_context(nc.Block())

        @block.sync
        def _(sp):
            for b in range(XB):
                sp.dma_start(acc[:, b * BT:(b + 1) * BT, :], x_tiles[b]).then_inc(x_loaded[b], 16)
            sp.dma_start(wqk_raw[:, :, :], wqk_in[0]).then_inc(wqk_loaded, 16)
            sp.dma_start(wv_raw[:, :, :], wv_in[0]).then_inc(wv_loaded, 16)
            sp.dma_start(wo_raw[:, :], wo_in[0]).then_inc(wo_loaded, 16)
            sp.dma_start(b1[:, :], b1_in).then_inc(consts_loaded, 16)
            sp.dma_start(b2[:, :], b2_in.partition_broadcast(P)).then_inc(consts_loaded, 16)

            def head_of(w, h):
                if isinstance(h, int):
                    return w[h]
                return w[bass.ds(h, 1)].squeeze(0)

            def query_key_weights(h):
                need(sp, wqk_split, h)
                sp.dma_start(wqk_raw[:, :, :], head_of(wqk_in, h)).then_inc(wqk_loaded, 16)

            def value_output_weights(h):
                need(sp, wv_split, h)
                sp.dma_start(wv_raw[:, :, :], head_of(wv_in, h)).then_inc(wv_loaded, 16)
                need(sp, wo_split, h)
                sp.dma_start(wo_raw[:, :], head_of(wo_in, h)).then_inc(wo_loaded, 16)

            query_key_weights(1)
            for i in range(2 * FFN_PIECES):
                need(sp, abs_done, i - 1)
                src = w1_pieces[i] if i < FFN_PIECES else w2_pieces[i - FFN_PIECES]
                sp.dma_start(ffn_raw[:, i % 2, :], src).then_inc(piece_loaded[i % 2], 16)

            with sp.Fori(2, HEADS) as h:
                query_key_weights(h)
                value_output_weights(h - 1)
            value_output_weights(LAST)
            sp.wait_ge(abs_done, 2 * FFN_PIECES)
            for i in range(2 * FFN_PIECES):
                need(sp, piece_done, i - 1)
                src = w1_pieces[i] if i < FFN_PIECES else w2_pieces[i - FFN_PIECES]
                sp.dma_start(ffn_raw[:, i % 2, :], src).then_inc(piece_loaded[i % 2], 16)
            for b in range(XB):
                need(sp, tr_ready, 2 * b - 2)
                sp.dma_start(x_stage[:, b % 2, :, :], x_tiles[b]).then_inc(x_again[b % 2], 16)
            for c in range(CHUNKS):
                sp.wait_ge(rows_done, c + 1)
                sp.dma_start(out_tiles[c], acc[:, 2 * c:2 * c + 2, :]).then_inc(y_stored, 16)
            sp.wait_ge(y_stored, 16 * CHUNKS)

        @block.gpsimd
        def _(pool):
            pool.memset(neg_half[:, :], -0.5).then_inc(const_made, 1)
            pool.memset(ones[:, :], 1.0).then_inc(const_made, 1)
            pool.memset(ident[:, :], 0.0).then_inc(const_made, 1)
            pool.wait_ge(const_made, 3)
            pool.affine_select(out=ident[:, :], in_=ident[:, :], compare_op=ALU.not_equal, fill=1.0, base=0,
                               pattern=[[-1, P]], channel_multiplier=1).then_inc(const_made, 1)

            def inverse_deviation(k, tiles):
                pool.wait_ge(ln_var, k + 1)
                n = tiles.stop - tiles.start
                pool.tensor_tensor(rstd[:, tiles], var_eps[:, tiles], neg_half[:, 0:n], ALU.pow).then_inc(ln_rstd, 1)

            def split(h, raw, hi, lo, loaded, hi_done, done):
                unit = ones[:, 0:1] if len(raw.shape) == 2 else ones[:, 0:1].unsqueeze(2)
                pool.wait_ge(loaded, 16 * (h + 1))
                pool.tensor_tensor(hi, raw, unit.broadcast_to(list(raw.shape)), ALU.mult).then_inc(hi_done, 1)
                pool.wait_ge(hi_done, h + 1)
                pool.tensor_tensor(lo, raw, hi.bitcast(F32), ALU.subtract).then_inc(done, 1)

            def split_query_key(h, par):
                split(h, wqk_raw[:, :, :], wqk_hi[:, par, :, :], wqk_lo[:, par, :, :], wqk_loaded, wqk_hi_done, wqk_split)

            def split_value_output(h, par):
                split(h, wv_raw[:, :, :], wv_hi[:, par, :, :], wv_lo[:, par, :, :], wv_loaded, wv_hi_done, wv_split)
                split(h, wo_raw[:, :], wo_hi[:, par, :], wo_lo[:, par, :], wo_loaded, wo_hi_done, wo_split)

            for b in range(XB):
                inverse_deviation(b, slice(b * BT, (b + 1) * BT))
            split_query_key(0, 0)
            pool.wait_ge(xn_ready, XB)
            pool.memset(acc[:, :, :], 0.0).then_inc(acc_zeroed, 1)
            split_query_key(1, 1)
            split_value_output(0, 0)

            def head(h, par, next_weights=True):
                for i in range(1, len(BY_POOL)):
                    pool.wait_ge(weighted_ready, len(BY_POOL) * h + (i + 1))
                    if i > 1:
                        pool.wait_ge(weighted_added, ADDS * h + (i - 1))
                    pool.tensor_tensor(weighted_sum[:, :], weighted[:, :], weighted_sum[:, :],
                                       ALU.add).then_inc(weighted_added, 1)
                    if BY_POOL[i] == 4 and not (isinstance(h, int) and h == 0):
                        pool.wait_ge(c_added, PE_SUMS * h)
                        split_value_output(h, par)
                    if BY_POOL[i] == 10 and next_weights:
                        pool.wait_ge(q_ready, 4 * h + 4)
                        split_query_key(h + 2, par)

            head(0, 0)
            head(1, 1)
            with pool.Fori(1, HEADS // 2 - 1) as it:
                head(2 * it, 0)
                head(2 * it + 1, 1)
            head(LAST - 1, 0, next_weights=False)
            pool.wait_ge(c_added, PE_SUMS * LAST)
            split_value_output(LAST, LAST % 2)

            pool.wait_ge(thresholds, 3)
            pool.wait_ge(s_ready, BANKS * UNITS * LAST)
            steps = 0
            for i in range(2 * FFN_PIECES):
                m = i // FFN_PIECES
                part = slice((i % FFN_PIECES) * BANK, (i % FFN_PIECES + 1) * BANK)
                hi = (k_hi[:, 0, :], w2_hi[:, :, :].rearrange("p f d -> p (f d)"))[m][:, part]
                lo = (k_lo[:, 0, :], w2_lo[:, :, :].rearrange("p f d -> p (f d)"))[m][:, part]
                raw = ffn_raw[:, i % 2, :]
                pool.wait_ge(piece_loaded[i % 2], 16 * (FFN_PIECES + i // 2 + 1))

                def then(ins):
                    nonlocal steps
                    steps += 1
                    ins.then_inc(quant_step, 1)
                    pool.wait_ge(quant_step, steps)

                then(pool.tensor_scalar(tmp[:, 0, :], raw, half_scale[:, m:m + 1], None, ALU.is_gt))
                then(pool.tensor_scalar(tmp[:, 1, :], raw, neg_half_scale[:, m:m + 1], None, ALU.is_lt))
                then(pool.tensor_tensor(tmp[:, 0, :], tmp[:, 0, :], tmp[:, 1, :], ALU.subtract))
                then(pool.tensor_tensor(tmp[:, 0, :], tmp[:, 0, :], raw, ALU.subtract))
                then(pool.tensor_tensor(tmp[:, 1, :], tmp[:, 0, :], raw, ALU.add))
                then(pool.tensor_copy(hi, tmp[:, 1, :]))
                pool.tensor_tensor(lo, tmp[:, 1, :], hi.bitcast(F32), ALU.subtract).then_inc(piece_done, 1)
                pool.wait_ge(piece_done, i + 1)
            sets = XB

            def deviations(tiles):
                nonlocal sets
                inverse_deviation(sets, tiles)
                sets += 1

            def both_norms(b):
                for _ in range(2):
                    deviations(slice(b * BT, (b + 1) * BT))

            def finish(c):
                deviations(slice(2 * c, 2 * c + 2))

            def split_hidden(c):
                for half in range(2):
                    fs = slice(half * FT // 2, (half + 1) * FT // 2)
                    pool.wait_ge(h_hi_done, 2 * c + half + 1)
                    need(pool, f_ready, c - 1)
                    h = hidden[:, c % 2, :].rearrange("p (f n) -> p f n", f=FT)[:, fs, :]
                    pool.tensor_tensor(hid_lo[:, c % 2, fs, :], h, hid_hi[:, c % 2, fs, :].bitcast(F32),
                                       ALU.subtract).then_inc(h_lo_done, 1)

            both_norms(0)
            both_norms(1)
            for c in range(CHUNKS):
                split_hidden(c)
                if c == 1:
                    both_norms(2)
                if c:
                    finish(c - 1)
                if c == 3:
                    both_norms(3)
            finish(CHUNKS - 1)

        @block.tensor
        def _(pe):
            def product(ps, pairs, first=True, last=True):
                n = 3 * len(pairs)
                i = 0
                for ah, al, bh, bl in pairs:
                    for a, b in ((ah, bh), (ah, bl), (al, bh)):
                        ins = pe.matmul(ps, a, b, start=first and i == 0, stop=last and i == n - 1)
                        i += 1
                return ins

            def project(ps, w_h, w_l, cols, chunk):
                toks = slice(chunk * BANK, (chunk + 1) * BANK)
                return product(ps, [(w_h[:, c, cols], w_l[:, c, cols], xt_hi[:, c, toks], xt_lo[:, c, toks])
                                    for c in range(HC)])

            def queries(ps, par, chunk):
                return project(ps, wqk_hi[:, par], wqk_lo[:, par], slice(0, D), chunk)

            def keys(ps, par, chunk):
                return project(ps, wqk_hi[:, par], wqk_lo[:, par], slice(D, 2 * D), chunk)

            pe.wait_ge(const_made, 4)
            for g in range(TILES // 2):
                pe.wait_ge(xn_ready, g // 2 + 1)
                need(pe, xt_lo_done, g - 3)
                for c in range(HC):
                    for t in range(2):
                        ins = pe.transpose(ps_s[:, g % 4, (2 * c + t) * P:(2 * c + t + 1) * P],
                                           xn[:, 2 * g + t, c * P:(c + 1) * P], ident[:, :])
                ins.then_inc(xt_ready, 1)
            pe.wait_ge(wqk_split, 1)
            for c in range(BANKS):
                pe.wait_ge(xt_lo_done, max(2 * c + 2, 4 + c + 1))
                keys(ps_s[:, c, :], 0, c).then_inc(k_ready, 1)
                if c == 0:
                    queries(ps_x[:, X_QUERIES, :], 0, 0).then_inc(q_ready, 1)

            def scores(h, par, r, bank):
                n = UNITS * h + r
                need(pe, exp_done, BANKS * (n - 1) + bank + 1)
                if bank == 0 and r % 4 == 0:
                    pe.wait_ge(q_lo_done, 4 * h + r // 4 + 1)
                if r == 0:
                    pe.wait_ge(k_lo_done, 4 * h + bank + 1)
                qs = slice((r % 4) * P, (r % 4 + 1) * P)
                ks = slice(bank * BANK, (bank + 1) * BANK)
                q = (r // 4) % 2
                product(ps_s[:, bank, :], [(q_hi[:, q, qs], q_lo[:, q, qs], k_hi[:, par, ks], k_lo[:, par, ks])])\
                    .then_inc(s_ready, 1)

            def sums_over_queries(n, u, start, stop):
                pe.wait_ge(rinv_ready, n + 1)
                for b in range(BANKS):
                    ins = pe.matmul(ps_c[32 * b:32 * b + 1, :], rinv[:, u % 2:u % 2 + 1],
                                    probs[:, u % 2, b * BANK:(b + 1) * BANK], start=start, stop=stop)
                ins.then_inc(c_added, 1)

            def sums_of_weighted(h):
                pe.wait_ge(weighted_added, ADDS * (h + 1))
                for b in range(BANKS):
                    ins = pe.matmul(ps_c[32 * b:32 * b + 1, :], ones[:, 0:1], weighted_sum[:, b * BANK:(b + 1) * BANK],
                                    start=False, stop=True)
                ins.then_inc(c_added, 1)

            def output(y, par):
                vb, x = (y // 2) % 2, X_ROWS[y % 2]
                for s in range(2):
                    ts = slice((y % 2) * CHUNK + s * P, (y % 2) * CHUNK + (s + 1) * P)
                    ins = product(ps_x[:, x, s * HID:(s + 1) * HID],
                                  [(v_hi[:, vb, ts], v_lo[:, vb, ts], wo_hi[:, par, :], wo_lo[:, par, :])])
                ins.then_inc(y_ready, 1)

            def sums(h, r, h0, last, after):
                n = UNITS * h + r
                first = 1 if last else 2
                if r == first and h0:
                    pe.wait_ge(c_cleared, 1)
                elif r == first:
                    pe.wait_ge(c_row_done, h)
                if r == 0 and not h0 or r > 0 and not after and (last or r - 1 not in BY_POOL):
                    sums_over_queries(n - 1, (r - 1) % UNITS, start=r == first, stop=after)
                if r == first - 1 and not h0 and not after:
                    sums_of_weighted(h - 1)

            def slot(h, par, r, h0=False, last=False, after=False):
                n, c = UNITS * h + r, r // 4
                if not after:
                    for bank in range(BANKS):
                        scores(h, par, r, bank)
                if r % 4 == 0 and not last and not after:
                    if r == 0:
                        pe.wait_ge(wqk_split, h + 2)
                    keys(ps_x[:, X_KEYS, :], 1 - par, c).then_inc(k_ready, 1)
                if r % 4 == 1 and not h0:
                    need(pe, y_used, YS * (h - 1) + 2 * c - 1)
                    if r == 1:
                        pe.wait_ge(wv_split, h)
                    project(ps_x[:, X_VALUES, :], wv_hi[:, 1 - par], wv_lo[:, 1 - par], slice(0, D), c).then_inc(v_ready, 1)
                if r % 4 == 2 and not after and not (last and c == 3):
                    if not last:
                        pe.wait_ge(k_lo_done, 4 * (h + 1) + c + 1)
                    queries(ps_x[:, X_QUERIES, :], par if c < 3 else 1 - par, (c + 1) % 4).then_inc(q_ready, 1)
                if r == 3 and not h0:
                    pe.wait_ge(c_row_done, h)
                    need(pe, y_used, YS * (h - 1))
                    for s in range(BANKS):
                        ins = pe.matmul(ps_x[:, X_COLUMNS, 4 * s:4 * s + 4], c_row[:, s * P:(s + 1) * P],
                                        ident[:, 0:P:32], start=True, stop=True)
                    ins.then_inc(c_turned, 1)
                if r % 4 == 3 and not h0:
                    pe.wait_ge(v_lo_done, 4 * (h - 1) + c + 1)
                    if r == 3:
                        pe.wait_ge(wo_split, h)
                    output(2 * c, 1 - par)
                    if c == 0:
                        pe.wait_ge(c_col_done, h)
                    else:
                        pe.wait_ge(y_used, YS * (h - 1) + 2 * c)
                    output(2 * c + 1, 1 - par)
                sums(h, r, h0, last, after)
                if h0 and r == 12:
                    pe.wait_ge(abs_done, 2 * FFN_PIECES + 2)
                    pe.matmul(ps_x[:, X_VALUES, 0:2], ones[:, :], abs_sum[:, :], start=True, stop=True)\
                        .then_inc(scale_ready, 1)
                if h0 and r == 15:
                    pe.wait_ge(thresholds, 1)

            def head(h, par, h0=False, last=False, after=False):
                for r in range(UNITS):
                    slot(h, par, r, h0, last, after)

            head(0, 0, h0=True)
            head(1, 1)
            with pe.Fori(1, HEADS // 2 - 1) as it:
                head(2 * it, 0)
                head(2 * it + 1, 1)
            head(LAST - 1, 0)
            head(LAST, 1, last=True)


            def turn_block_input(b):
                pe.wait_ge(xn_ready, XB + b + 1)
                for g in range(2 * b, 2 * b + 2):
                    need(pe, tr_lo_done, g - 1)
                    for c in range(HC):
                        for t in range(2):
                            ins = pe.transpose(ps_turned[g % 2][:, (2 * c + t) * P:(2 * c + t + 1) * P],
                                               x_stage[:, b % 2, (2 * g + t) % BT, c * P:(c + 1) * P], ident[:, :])
                    ins.then_inc(tr_ready, 1)

            def up(c):
                pe.wait_ge(tr_lo_done, c + 1)
                toks = slice(c * CHUNK, (c + 1) * CHUNK)
                for f in range(FT):
                    if f % 2 == 0:
                        need(pe, gelu_done, FT * (c - 1) + f + 2)
                    fs = slice(f * P, (f + 1) * P)
                    product(ps_s[:, f // 2, (f % 2) * CHUNK:(f % 2 + 1) * CHUNK],
                            [(w1_hi[:, k, fs], w1_lo[:, k, fs], xt_hi[:, k, toks], xt_lo[:, k, toks]) for k in range(HC)])\
                        .then_inc(h_ready, 1)

            def down(c):
                pe.wait_ge(h_lo_done, 2 * c + 2)
                need(pe, f_used, c - 1)
                for t in range(2):
                    ts = slice(t * P, (t + 1) * P)
                    ins = product(ps_f[c % 2][:, t * HID:(t + 1) * HID],
                                  [(hid_hi[:, c % 2, f, ts], hid_lo[:, c % 2, f, ts], w2_hi[:, f, :], w2_lo[:, f, :])
                                   for f in range(FT)])
                ins.then_inc(f_ready, 1)

            for r in range(10):
                slot(HEADS, 0, r, after=True)
            turn_block_input(0)
            pe.wait_ge(piece_done, FFN_PIECES)
            up(0)
            slot(HEADS, 0, 11, after=True)
            up(1)
            slot(HEADS, 0, 13, after=True)
            turn_block_input(1)
            slot(HEADS, 0, 15, after=True)
            pe.wait_ge(piece_done, 2 * FFN_PIECES)
            pe.wait_ge(y_used, YS * HEADS)
            down(0)
            up(2)
            for c in range(2, CHUNKS):
                if c % 2 and (c + 1) // 2 < XB:
                    turn_block_input((c + 1) // 2)
                if c:
                    down(c - 1)
                if c + 1 < CHUNKS:
                    up(c + 1)
            down(CHUNKS - 1)

        @block.scalar
        def _(act):
            for g in range(TILES // 2):
                act.wait_ge(xt_ready, g + 1)
                act.activation(xt_hi[:, :, g * CHUNK:(g + 1) * CHUNK],
                               ps_s[:, g % 4, :].rearrange("p (c n) -> p c n", c=HC), ACT.Copy).then_inc(xt_hi_done, 1)

            def keys(h, par, c, src):
                act.wait_ge(k_ready, 4 * h + c + 1)
                act.activation(k_hi[:, par, c * BANK:(c + 1) * BANK], src, ACT.Copy).then_inc(k_hi_done, 1)

            def queries(h, c):
                act.wait_ge(q_ready, 4 * h + c + 1)
                act.activation(q_hi[:, c % 2, :], ps_x[:, X_QUERIES, :], ACT.Copy, scale=SCALE).then_inc(q_hi_done, 1)

            for c in range(BANKS):
                keys(0, 0, c, ps_s[:, c, :])
                if c == 0:
                    queries(0, 0)

            def exp_unit(n, r):
                act.wait_ge(max_ready, n + 1)
                for b in range(BANKS):
                    act.activation(probs[:, r % 2, b * BANK:(b + 1) * BANK], ps_s[:, b, :], ACT.Exp,
                                   bias=negmax[:, r % 2:r % 2 + 1], scale=1.0,
                                   accum_out=rowsum[:, r % 2, b:b + 1]).then_inc(exp_done, 1)

            def weigh(h, u):
                i = BY_POOL.index(u)
                act.wait_ge(rinv_ready, UNITS * h + (u + 1))
                if i > 1:
                    act.wait_ge(weighted_added, ADDS * h + (i - 1))
                act.activation((weighted if i else weighted_sum)[:, :], probs[:, u % 2, :], ACT.Copy,
                               scale=rinv[:, u % 2:u % 2 + 1]).then_inc(weighted_ready, 1)

            def slot(h, par, r, h0=False, last=False, after=False):
                c = r // 4
                if r == (1 if last or after else 2) and not h0:
                    act.wait_ge(c_added, PE_SUMS * LAST + UNITS if after else PE_SUMS * h)
                    need(act, c_turned, h - 1)
                    act.activation(c_row[:, :], ps_c[:, :], ACT.Copy).then_inc(c_row_done, 1)
                if r % 4 == 1 and not last and not after:
                    keys(h + 1, 1 - par, c, ps_x[:, X_KEYS, :])
                if r % 4 == 3 and not after and not (last and c == 3):
                    queries(h, c + 1)
                if not last and not after and r - 2 in BY_POOL:
                    weigh(h, r - 2)
                    act.wait_ge(weighted_ready, len(BY_POOL) * h + BY_POOL.index(r - 2) + 1)
                if not after:
                    exp_unit(UNITS * h + r, r)

            def head(h, par, h0=False, last=False, after=False):
                for r in range(UNITS):
                    slot(h, par, r, h0, last, after)

            head(0, 0, h0=True)
            head(1, 1)
            with act.Fori(1, HEADS // 2 - 1) as it:
                head(2 * it, 0)
                head(2 * it + 1, 1)
            head(LAST - 1, 0)
            head(LAST, 1, last=True)
            head(HEADS, 0, after=True)

            act.wait_ge(consts_loaded, 32)

            def split_turned(g):
                act.wait_ge(tr_ready, g + 1)
                act.activation(xt_hi[:, :, g * CHUNK:(g + 1) * CHUNK],
                               ps_turned[g % 2].rearrange("p (c n) -> p c n", c=HC), ACT.Copy).then_inc(tr_hi_done, 1)

            split_turned(0)
            split_turned(1)
            for c in range(CHUNKS):
                need(act, h_lo_done, 2 * c - 2)
                for f in range(FT):
                    if f % 2 == 0:
                        act.wait_ge(h_ready, FT * c + f + 2)
                    act.activation(hidden[:, c % 2, f * CHUNK:(f + 1) * CHUNK],
                                   ps_s[:, f // 2, (f % 2) * CHUNK:(f % 2 + 1) * CHUNK], ACT.Gelu,
                                   bias=b1[:, f:f + 1], scale=1.0).then_inc(gelu_done, 1)
                    if f % (FT // 2) == FT // 2 - 1:
                        act.wait_ge(gelu_done, FT * c + f + 1)
                        need(act, f_ready, c - 1)
                        half = slice(f + 1 - FT // 2, f + 1)
                        act.activation(hid_hi[:, c % 2, half, :],
                                       hidden[:, c % 2, half.start * CHUNK:half.stop * CHUNK]
                                       .rearrange("p (f n) -> p f n", n=CHUNK), ACT.Copy).then_inc(h_hi_done, 1)
                if c % 2 and (c + 1) // 2 < XB:
                    split_turned(c + 1)
                    split_turned(c + 2)

        @block.vector
        def _(dve):
            ln_steps = 0

            def variances(sets, tiles, src, wait_src=None):
                nonlocal ln_steps
                for i, t in enumerate(tiles):
                    dve.bn_stats(stats[:, i, :], src(t)).then_inc(ln_step, 1)
                    ln_steps += 1
                first = ln_steps - len(tiles)
                for i, t in enumerate(tiles):
                    dve.wait_ge(ln_step, first + i + 1)
                    dve.bn_aggr(mv[:, t, :], stats[:, i, :]).then_inc(ln_step, 1)
                    ln_steps += 1
                dve.wait_ge(ln_step, ln_steps)
                a, b = tiles[0], tiles[-1] + 1
                dve.tensor_scalar(var_eps[:, a:b], mv[:, a:b, 1], LN_EPS, None, ALU.add).then_inc(ln_var, 1)

            def normalise(dst, src, t):
                return dve.tensor_scalar(dst, src, mv[:, t, 0:1], rstd[:, t:t + 1], ALU.subtract, ALU.mult)

            batch = [list(range(b * BT, (b + 1) * BT)) for b in range(XB)]

            def normalise_input(b):
                dve.wait_ge(ln_rstd, b + 1)
                for t in batch[b]:
                    ins = normalise(xn[:, t, :], acc[:, t, :], t)
                ins.then_inc(xn_ready, 1)

            for b in range(XB):
                dve.wait_ge(x_loaded[b], 16)
                if b:
                    dve.wait_ge(ln_step, ln_steps)
                variances(b, batch[b], lambda t: acc[:, t, :])
                if b:
                    normalise_input(b - 1)
            normalise_input(XB - 1)

            for g in range(TILES // 2):
                dve.wait_ge(xt_hi_done, g + 1)
                hi = xt_hi[:, :, g * CHUNK:(g + 1) * CHUNK]
                dve.tensor_tensor(xt_lo[:, :, g * CHUNK:(g + 1) * CHUNK],
                                  ps_s[:, g % 4, :].rearrange("p (c n) -> p c n", c=HC), hi.bitcast(F32),
                                  ALU.subtract).then_inc(xt_lo_done, 1)

            dve.memset(ps_c[:, :], 0.0).then_inc(c_cleared, 1)

            def keys(h, par, c, src):
                dve.wait_ge(k_hi_done, 4 * h + c + 1)
                ks = slice(c * BANK, (c + 1) * BANK)
                dve.tensor_tensor(k_lo[:, par, ks], src, k_hi[:, par, ks].bitcast(F32), ALU.subtract).then_inc(k_lo_done, 1)

            def queries(h, c):
                dve.wait_ge(q_hi_done, 4 * h + c + 1)
                dve.scalar_tensor_tensor(out=q_lo[:, c % 2, :], in0=ps_x[:, X_QUERIES, :], scalar=SCALE,
                                         in1=q_hi[:, c % 2, :].bitcast(F32), op0=ALU.mult, op1=ALU.subtract)\
                    .then_inc(q_lo_done, 1)

            for c in range(BANKS):
                keys(0, 0, c, ps_s[:, c, :])
                if c == 0:
                    queries(0, 0)

            def sum_magnitudes(i):
                dve.wait_ge(piece_loaded[i % 2], 16 * (i // 2 + 1))
                dve.tensor_reduce(abs_piece[:, i:i + 1], ffn_raw[:, i % 2, :], AX_X, ALU.add,
                                  apply_absolute_value=True).then_inc(abs_done, 1)

            def sum_pieces():
                dve.wait_ge(abs_done, 2 * FFN_PIECES)
                for m in range(2):
                    dve.tensor_reduce(abs_sum[:, m:m + 1], abs_piece[:, m * FFN_PIECES:(m + 1) * FFN_PIECES], AX_X,
                                      ALU.add).then_inc(abs_done, 1)

            def make_thresholds():
                dve.wait_ge(scale_ready, 1)
                dve.tensor_scalar(scale[:, :], ps_x[:, X_VALUES, 0:2], 1.0 / (HID * DFF), QUANT_EPS, ALU.mult, ALU.max)\
                    .then_inc(thresholds, 1)
                dve.wait_ge(thresholds, 1)
                dve.tensor_scalar(half_scale[:, :], scale[:, :], 0.5, None, ALU.mult).then_inc(thresholds, 1)
                dve.tensor_scalar(neg_half_scale[:, :], scale[:, :], -0.5, None, ALU.mult).then_inc(thresholds, 1)

            def bank_max(n, r, bank):
                dve.wait_ge(s_ready, 4 * n + bank + 1)
                dve.tensor_reduce(qmax[:, r % 2, bank:bank + 1], ps_s[:, bank, :], AX_X, ALU.max).then_inc(qmax_done, 1)

            def row_max(n, r):
                dve.wait_ge(qmax_done, 4 * n + BANKS)
                dve.tensor_reduce(negmax[:, r % 2:r % 2 + 1], qmax[:, r % 2, :], AX_X, ALU.max,
                                  negate=True).then_inc(max_ready, 1)

            def row_sum(n, u):
                dve.wait_ge(exp_done, BANKS * (n + 1))
                dve.tensor_reduce(total[:, u % 2:u % 2 + 1], rowsum[:, u % 2, :], AX_X, ALU.add).then_inc(sum_step, 1)
                dve.wait_ge(sum_step, n + 1)
                dve.reciprocal(rinv[:, u % 2:u % 2 + 1], total[:, u % 2:u % 2 + 1]).then_inc(rinv_ready, 1)

            def add_rows(h, y):
                dve.wait_ge(y_ready, YS * h + y + 1)
                if y == 0:
                    dve.wait_ge(c_col_done, h + 1)
                    dve.wait_ge(acc_zeroed, 1)
                need(dve, y_used, YS * h + y)
                for s in range(2):
                    tile = 2 * y + s
                    a, b = tile % BANKS, tile // BANKS
                    ins = dve.scalar_tensor_tensor(out=acc[:, tile, :], in0=ps_x[:, X_ROWS[y % 2], s * HID:(s + 1) * HID],
                                                   scalar=c_col[:, a, b:b + 1], in1=acc[:, tile, :],
                                                   op0=ALU.mult, op1=ALU.add)
                ins.then_inc(y_used, 1)

            def values(h, c):
                dve.wait_ge(v_ready, 4 * h + c + 1)
                need(dve, y_ready, YS * h + 2 * c - 2)
                dve.tensor_copy(v_hi[:, c % 2, :], ps_x[:, X_VALUES, :]).then_inc(v_hi_done, 1)
                dve.wait_ge(v_hi_done, 4 * h + c + 1)
                dve.tensor_tensor(v_lo[:, c % 2, :], ps_x[:, X_VALUES, :], v_hi[:, c % 2, :].bitcast(F32),
                                  ALU.subtract).then_inc(v_lo_done, 1)

            def slot(h, par, r, h0=False, last=False, after=False):
                n, c = UNITS * h + r, r // 4
                sum_now = (last or r - 1 not in BY_POOL) and not after and not (h0 and r == 0)
                sum_later = not sum_now and (r > 0 and not after or after and r == 0)
                if not after:
                    bank_max(n, r, 0)
                    bank_max(n, r, 1)
                    if sum_now:
                        row_sum(n - 1, (r - 1) % UNITS)
                    bank_max(n, r, 2)
                    bank_max(n, r, 3)
                    row_max(n, r)
                if r == 3 and not h0:
                    dve.wait_ge(c_turned, h)
                    need(dve, y_used, YS * (h - 1))
                    dve.tensor_copy(c_col[:, :, :], ps_x[:, X_COLUMNS, 0:16].rearrange("p (a b) -> p a b", a=BANKS))\
                        .then_inc(c_col_done, 1)
                if r % 4 == 3 and not after and not (last and c == 3):
                    queries(h, c + 1)
                if sum_later:
                    row_sum(n - 1, (r - 1) % UNITS)
                if r % 4 == 0 and not h0 and (r > 0 or not isinstance(h, int) or h > 1):
                    pair(h - 1 if r else h - 2, (2 * c - 2) % YS)
                if r % 4 == 1 and not last and not after:
                    keys(h + 1, 1 - par, c, ps_x[:, X_KEYS, :])
                if r % 4 == 2 and not h0:
                    values(h - 1, c)

            def pair(h, y):
                add_rows(h, y)
                add_rows(h, y + 1)

            def head(h, par, h0=False, last=False, after=False):
                for r in range(UNITS):
                    slot(h, par, r, h0, last, after)
                    if h0 and 2 <= r < 2 + 2 * FFN_PIECES:
                        sum_magnitudes(r - 2)
                    if h0 and r == 2 + 2 * FFN_PIECES:
                        sum_pieces()
                    if h0 and r == 12:
                        make_thresholds()

            head(0, 0, h0=True)
            head(1, 1)
            with dve.Fori(1, HEADS // 2 - 1) as it:
                head(2 * it, 0)
                head(2 * it + 1, 1)
            head(LAST - 1, 0)
            head(LAST, 1, last=True)
            for r in range(5):
                slot(HEADS, 0, r, after=True)

            sets = XB

            def deviations(tiles, src):
                nonlocal sets
                dve.wait_ge(ln_step, ln_steps)
                variances(sets, tiles, src)
                sets += 1
                dve.wait_ge(ln_rstd, sets)

            def then(ins):
                nonlocal local_steps
                local_steps += 1
                ins.then_inc(local_step, 1)

            def settled():
                dve.wait_ge(local_step, local_steps)

            local_steps = 0

            def attention_stats(b):
                nonlocal sets
                dve.wait_ge(y_used, YS * LAST + 2 * (b + 1))
                dve.wait_ge(ln_step, ln_steps)
                variances(sets, batch[b], lambda t: acc[:, t, :])
                sets += 1

            def attention_norm(b):
                nonlocal sets
                dve.wait_ge(ln_rstd, sets)
                for t in batch[b]:
                    then(normalise(acc[:, t, :], acc[:, t, :], t))
                dve.wait_ge(x_again[b % 2], 16 * (b // 2 + 1))
                settled()
                for t in batch[b]:
                    then(dve.tensor_tensor(acc[:, t, :], acc[:, t, :], x_stage[:, b % 2, t % BT, :], ALU.add))
                settled()
                variances(sets, batch[b], lambda t: acc[:, t, :])
                sets += 1

            def input_norm(b):
                dve.wait_ge(ln_rstd, sets)
                for t in batch[b]:
                    ins = normalise(x_stage[:, b % 2, t % BT, :], acc[:, t, :], t)
                ins.then_inc(xn_ready, 1)

            def split_turned(g):
                dve.wait_ge(tr_hi_done, g + 1)
                toks = slice(g * CHUNK, (g + 1) * CHUNK)
                dve.tensor_tensor(xt_lo[:, :, toks], ps_turned[g % 2].rearrange("p (c n) -> p c n", c=HC),
                                  xt_hi[:, :, toks].bitcast(F32), ALU.subtract).then_inc(tr_lo_done, 1)

            def finish(c):
                dve.wait_ge(f_ready, c + 1)
                need(dve, rows_done, c)
                ffn = tmp[:, 0, :].rearrange("p (t d) -> p t d", t=2)
                for t in range(2):
                    ins = dve.tensor_tensor(ffn[:, t, :], ps_f[c % 2][:, t * HID:(t + 1) * HID], b2[:, :], ALU.add)
                ins.then_inc(f_used, 1)
                dve.wait_ge(f_used, c + 1)
                deviations([2 * c, 2 * c + 1], lambda t: ffn[:, t % 2, :])
                for t in range(2):
                    then(normalise(ffn[:, t, :], ffn[:, t, :], 2 * c + t))
                settled()
                tiles = slice(2 * c, 2 * c + 2)
                dve.tensor_tensor(acc[:, tiles, :], acc[:, tiles, :], ffn, ALU.add).then_inc(rows_done, 1)

            attention_stats(0)
            values(LAST, 1)
            attention_norm(0)
            pair(LAST, 2)
            input_norm(0)
            attention_stats(1)
            split_turned(0)
            split_turned(1)
            values(LAST, 2)
            attention_norm(1)
            input_norm(1)
            pair(LAST, 4)
            values(LAST, 3)
            attention_stats(2)
            pair(LAST, 6)
            split_turned(2)
            split_turned(3)
            attention_norm(2)
            input_norm(2)
            dve.wait_ge(consts_loaded, 32)
            for c in range(CHUNKS):
                if c % 2 and 1 < (c + 1) // 2 < XB:
                    split_turned(c + 1)
                    split_turned(c + 2)
                if c:
                    finish(c - 1)
                if c == 3:
                    attention_stats(3)
                    attention_norm(3)
                    input_norm(3)
            finish(CHUNKS - 1)


def kernel(L0_attn_x, L0_attn_w_qkv, L0_attn_w_o, L0_ffn_w1, L0_ffn_b1, L0_ffn_w2, L0_ffn_b2):
    import numpy as np
    import concourse.bacc as bacc
    from concourse.bass_utils import run_bass_kernel_spmd

    x = np.asarray(L0_attn_x)
    batch, tokens, hid = x.shape
    d = P
    heads = L0_attn_w_o.shape[0] // d
    dff = L0_ffn_w1.shape[0]
    hc = hid // P
    w_qkv = np.asarray(L0_attn_w_qkv).reshape(hc, P, 3, heads, d)
    arrays = {
        "x": x.reshape(batch * tokens, hid),
        "w_qk": w_qkv[:, :, 0:2].transpose(3, 1, 0, 2, 4).reshape(heads, P, hc, 2 * d),
        "w_v": w_qkv[:, :, 2].transpose(2, 1, 0, 3),
        "w_o": np.asarray(L0_attn_w_o).reshape(heads, d, hid),
        "w1": np.asarray(L0_ffn_w1).T.reshape(hc, P, dff).transpose(1, 0, 2),
        "b1": np.asarray(L0_ffn_b1).reshape(dff // P, P).T,
        "w2": np.asarray(L0_ffn_w2).T.reshape(dff // P, P, hid).transpose(1, 0, 2),
        "b2": np.asarray(L0_ffn_b2),
    }
    arrays = {f"in_{k}": np.ascontiguousarray(v) for k, v in arrays.items()}
    nc = bacc.Bacc("TRN2", target_bir_lowering=False, num_devices=1)
    ins = [nc.dram_tensor(k, v.shape, mybir.dt.from_np(v.dtype), kind="ExternalInput").ap() for k, v in arrays.items()]
    out = nc.dram_tensor("out", (batch * tokens, hid), F32, kind="ExternalOutput").ap()
    sandwich_block(nc, *ins, out)
    result = run_bass_kernel_spmd(nc, [arrays], core_ids=[0])
    return result.results[0]["out"].reshape(batch, tokens, hid)
```

```python
from contextlib import ExitStack

import concourse.bass as bass
from concourse import mybir

F32 = mybir.dt.float32
F32R = mybir.dt.float32r
ALU = mybir.AluOpType
ACT = mybir.ActivationFunctionType
AX_X = mybir.AxisListType.X

P = 128
BANK = 512
LN_EPS = 1e-5
QUANT_EPS = 1e-8


def need(eng, sem, count):
    if isinstance(count, int) and count <= 0:
        return
    eng.wait_ge(sem, count)


def sandwich_block(nc, x_in, wqk_in, wv_in, wo_in, w1_in, b1_in, w2_in, b2_in, out):
    TOKENS, HID = x_in.shape
    HEADS, _, HC, D = wv_in.shape
    DFF = w1_in.shape[2]
    TILES = TOKENS // P
    UNITS = TILES
    BANKS = TOKENS // BANK
    FT = DFF // P
    LAST = HEADS - 1
    SCALE = float(D) ** -0.5
    assert D == P and HID == HC * P and UNITS == 4 * BANKS and BANKS == 4 and HEADS % 2 == 0

    YS = TILES // 2
    XB = 4
    BT = TILES // XB
    FFN_PIECES = HC * DFF // BANK
    CHUNK = 2 * P
    CHUNKS = TOKENS // CHUNK
    EARLY = 1
    PIECE_ORDER = [FFN_PIECES + i for i in range(EARLY)] + list(range(FFN_PIECES)) \
        + [FFN_PIECES + i for i in range(EARLY, FFN_PIECES)]
    BY_POOL = list(range(1, UNITS - 2, 2))
    ADDS = len(BY_POOL) - 1
    SHARED = [u for u in BY_POOL if u % 4 == 1]
    ACT_KEYS = (BANKS - 1) * BANK
    PE_SUMS = UNITS - len(BY_POOL) + 1

    with ExitStack() as ctx:
        def sb(name, shape, dt=F32):
            return ctx.enter_context(nc.sbuf_tensor(name, shape, dt))

        def sem(name):
            return ctx.enter_context(nc.semaphore(name))

        xt_hi = sb("xt_hi", [P, HC, TOKENS], F32R)
        xt_lo = sb("xt_lo", [P, HC, TOKENS], F32R)
        k_hi = sb("k_hi", [P, 2, TOKENS], F32R)
        k_lo = sb("k_lo", [P, 2, TOKENS], F32R)
        q_hi = sb("q_hi", [P, 2, BANK], F32R)
        q_lo = sb("q_lo", [P, 2, BANK], F32R)
        v_hi = sb("v_hi", [P, 2, BANK], F32R)
        v_lo = sb("v_lo", [P, 2, BANK], F32R)
        probs = sb("probs", [P, 2, TOKENS])
        acc = sb("acc", [P, TILES, HID])
        wqk_hi = sb("wqk_hi", [P, 2, HC, 2 * D], F32R)
        wqk_lo = sb("wqk_lo", [P, 2, HC, 2 * D], F32R)
        wqk_raw = sb("wqk_raw", [P, HC, 2 * D])
        wv_hi = sb("wv_hi", [P, 2, HC, D], F32R)
        wv_lo = sb("wv_lo", [P, 2, HC, D], F32R)
        wv_raw = sb("wv_raw", [P, HC, D])
        wo_hi = sb("wo_hi", [P, 2, HID], F32R)
        wo_lo = sb("wo_lo", [P, 2, HID], F32R)
        wo_raw = sb("wo_raw", [P, HID])
        w2_hi = sb("w2_hi", [P, FT, HID], F32R)
        w2_lo = sb("w2_lo", [P, FT, HID], F32R)
        hid_hi = sb("hid_hi", [P, 2, FT, CHUNK], F32R)
        with nc.sbuf_tensor("weighted_sum", [P, TOKENS], F32) as weighted_sum, \
                nc.sbuf_tensor("weighted", [P, TOKENS], F32) as weighted:
            pass
        hid_lo = sb("hid_lo", [P, 2, FT, CHUNK], F32R)
        c_row = sb("c_row", [P, BANK])
        c_col = sb("c_col", [P, BANKS, BANKS])
        tmp = sb("tmp", [P, 2, BANK])
        ffn_raw = sb("ffn_raw", [P, 2, BANK])
        x_stage = sb("x_stage", [P, 2, BT, HID])
        ident = sb("ident", [P, P])
        ones = sb("ones", [P, P])
        b1 = sb("b1", [P, FT])
        b2 = sb("b2", [P, HID])
        qmax = sb("qmax", [P, 2, BANKS])
        negmax = sb("negmax", [P, 2])
        rowsum = sb("rowsum", [P, 2, BANKS])
        total = sb("total", [P, 2])
        rinv = sb("rinv", [P, 2])
        stats = sb("stats", [P, BT, 6])
        mv = sb("mv", [P, TILES, 2])
        var_eps = sb("var_eps", [P, TILES])
        rstd = sb("rstd", [P, TILES])
        neg_half = sb("neg_half", [P, BT])
        abs_piece = sb("abs_piece", [P, 2 * FFN_PIECES])
        scale = sb("scale", [P, 2])
        abs_sum = sb("abs_sum", [P, 2])
        half_scale = sb("half_scale", [P, 2])
        neg_half_scale = sb("neg_half_scale", [P, 2])
        xn = probs[:, :, :].rearrange("p a (t d) -> p (a t) d", d=HID)
        w1_hi = k_hi[:, 0, :].rearrange("p (c f) -> p c f", c=HC)
        w1_lo = k_lo[:, 0, :].rearrange("p (c f) -> p c f", c=HC)
        hidden = probs

        ps_s = ctx.enter_context(nc.psum_tensor("ps_s", [P, BANKS + 1, BANK], F32))
        ps_c = ctx.enter_context(nc.psum_tensor("ps_c", [P, BANK], F32))
        ps_x = ctx.enter_context(nc.psum_tensor("ps_x", [P, 2, BANK], F32))
        X_VALUES, X_KEYS = 0, 1
        X_ROWS, X_QUERIES = X_VALUES, X_KEYS
        SPARE = BANKS
        ps_turned = [ps_x[:, X_KEYS, :], ps_c[:, :]]
        ps_f = [ps_s[:, SPARE, :], ps_x[:, X_VALUES, :]]

        def score_bank(r, bank):
            return SPARE if bank == 0 and r % 2 else bank

        x_loaded = [sem(f"x_loaded{b}") for b in range(XB)]
        consts_loaded = sem("consts_loaded")
        wqk_loaded = sem("wqk_loaded")
        wv_loaded = sem("wv_loaded")
        wo_loaded = sem("wo_loaded")
        const_made = sem("const_made")
        ln_var = sem("ln_var")
        ln_rstd = sem("ln_rstd")
        ln_step = sem("ln_step")
        xn_ready = sem("xn_ready")
        xt_ready = sem("xt_ready")
        xt_hi_done = sem("xt_hi_done")
        xt_lo_done = sem("xt_lo_done")
        abs_done = sem("abs_done")
        scale_ready = sem("scale_ready")
        acc_zeroed = sem("acc_zeroed")
        thresholds = sem("thresholds")
        wqk_hi_done = sem("wqk_hi_done")
        wqk_split = sem("wqk_split")
        wv_hi_done = sem("wv_hi_done")
        wv_split = sem("wv_split")
        wo_hi_done = sem("wo_hi_done")
        wo_split = sem("wo_split")
        c_cleared = sem("c_cleared")
        s_ready = sem("s_ready")
        qmax_done = sem("qmax_done")
        max_ready = sem("max_ready")
        exp_done = sem("exp_done")
        rinv_ready = sem("rinv_ready")
        c_added = sem("c_added")
        weighted_ready = sem("weighted_ready")
        weighted_added = sem("weighted_added")
        bank_weighted = sem("bank_weighted")
        c_row_done = sem("c_row_done")
        c_turned = sem("c_turned")
        c_col_done = sem("c_col_done")
        k_ready = sem("k_ready")
        k_hi_done = sem("k_hi_done")
        k_lo_done = sem("k_lo_done")
        q_ready = sem("q_ready")
        q_hi_done = sem("q_hi_done")
        q_lo_done = sem("q_lo_done")
        v_ready = sem("v_ready")
        v_hi_done = sem("v_hi_done")
        v_lo_done = sem("v_lo_done")
        y_ready = sem("y_ready")
        y_used = sem("y_used")
        sum_step = sem("sum_step")
        piece_loaded = [sem(f"piece_loaded{i}") for i in range(2)]
        quant_step = sem("quant_step")
        piece_done = sem("piece_done")
        x_again = [sem(f"x_again{i}") for i in range(2)]
        tr_ready = sem("tr_ready")
        tr_hi_done = sem("tr_hi_done")
        tr_lo_done = sem("tr_lo_done")
        h_ready = sem("h_ready")
        gelu_done = sem("gelu_done")
        h_hi_done = sem("h_hi_done")
        h_lo_done = sem("h_lo_done")
        f_ready = sem("f_ready")
        f_used = sem("f_used")
        local_step = sem("local_step")
        rows_done = sem("rows_done")
        y_stored = sem("y_stored")

        x_tiles = x_in.rearrange("(b t p) d -> b p t d", b=XB, p=P)
        out_tiles = out.rearrange("(c t p) d -> c p t d", t=2, p=P)
        w1_pieces = w1_in.rearrange("p c (s n) -> (c s) p n", n=BANK)
        w2_pieces = w2_in.rearrange("p (s f) d -> s p (f d)", f=BANK // HID)


        block = ctx.enter_context(nc.Block())

        @block.sync
        def _(sp):
            for b in range(XB):
                sp.dma_start(acc[:, b * BT:(b + 1) * BT, :], x_tiles[b]).then_inc(x_loaded[b], 16)
            sp.dma_start(wqk_raw[:, :, :], wqk_in[0]).then_inc(wqk_loaded, 16)
            sp.dma_start(wv_raw[:, :, :], wv_in[0]).then_inc(wv_loaded, 16)
            sp.dma_start(wo_raw[:, :], wo_in[0]).then_inc(wo_loaded, 16)
            sp.dma_start(b1[:, :], b1_in).then_inc(consts_loaded, 16)
            sp.dma_start(b2[:, :], b2_in.partition_broadcast(P)).then_inc(consts_loaded, 16)

            def head_of(w, h):
                if isinstance(h, int):
                    return w[h]
                return w[bass.ds(h, 1)].squeeze(0)

            def query_key_weights(h):
                need(sp, wqk_split, h)
                sp.dma_start(wqk_raw[:, :, :], head_of(wqk_in, h)).then_inc(wqk_loaded, 16)

            def value_output_weights(h):
                need(sp, wv_split, h)
                sp.dma_start(wv_raw[:, :, :], head_of(wv_in, h)).then_inc(wv_loaded, 16)
                need(sp, wo_split, h)
                sp.dma_start(wo_raw[:, :], head_of(wo_in, h)).then_inc(wo_loaded, 16)

            query_key_weights(1)
            for i in range(2 * FFN_PIECES):
                need(sp, abs_done, i - 1)
                src = w1_pieces[i] if i < FFN_PIECES else w2_pieces[i - FFN_PIECES]
                sp.dma_start(ffn_raw[:, i % 2, :], src).then_inc(piece_loaded[i % 2], 16)

            with sp.Fori(2, HEADS) as h:
                query_key_weights(h)
                value_output_weights(h - 1)
            value_output_weights(LAST)
            sp.wait_ge(abs_done, 2 * FFN_PIECES)
            for i, piece in enumerate(PIECE_ORDER):
                need(sp, piece_done, i - 1)
                src = w1_pieces[piece] if piece < FFN_PIECES else w2_pieces[piece - FFN_PIECES]
                sp.dma_start(ffn_raw[:, i % 2, :], src).then_inc(piece_loaded[i % 2], 16)
            for b in range(XB):
                need(sp, tr_ready, 2 * b - 2)
                sp.dma_start(x_stage[:, b % 2, :, :], x_tiles[b]).then_inc(x_again[b % 2], 16)
            for c in range(CHUNKS):
                sp.wait_ge(rows_done, c + 1)
                sp.dma_start(out_tiles[c], acc[:, 2 * c:2 * c + 2, :]).then_inc(y_stored, 16)
            sp.wait_ge(y_stored, 16 * CHUNKS)

        @block.gpsimd
        def _(pool):
            pool.memset(neg_half[:, :], -0.5).then_inc(const_made, 1)
            pool.memset(ones[:, :], 1.0).then_inc(const_made, 1)
            pool.memset(ident[:, :], 0.0).then_inc(const_made, 1)
            pool.wait_ge(const_made, 3)
            pool.affine_select(out=ident[:, :], in_=ident[:, :], compare_op=ALU.not_equal, fill=1.0, base=0,
                               pattern=[[-1, P]], channel_multiplier=1).then_inc(const_made, 1)

            def inverse_deviation(k, tiles):
                pool.wait_ge(ln_var, k + 1)
                n = tiles.stop - tiles.start
                pool.tensor_tensor(rstd[:, tiles], var_eps[:, tiles], neg_half[:, 0:n], ALU.pow).then_inc(ln_rstd, 1)

            def split(h, raw, hi, lo, loaded, hi_done, done):
                unit = ones[:, 0:1] if len(raw.shape) == 2 else ones[:, 0:1].unsqueeze(2)
                pool.wait_ge(loaded, 16 * (h + 1))
                pool.tensor_tensor(hi, raw, unit.broadcast_to(list(raw.shape)), ALU.mult).then_inc(hi_done, 1)
                pool.wait_ge(hi_done, h + 1)
                pool.tensor_tensor(lo, raw, hi.bitcast(F32), ALU.subtract).then_inc(done, 1)

            def split_query_key(h, par):
                split(h, wqk_raw[:, :, :], wqk_hi[:, par, :, :], wqk_lo[:, par, :, :], wqk_loaded, wqk_hi_done, wqk_split)

            def split_value_output(h, par):
                split(h, wv_raw[:, :, :], wv_hi[:, par, :, :], wv_lo[:, par, :, :], wv_loaded, wv_hi_done, wv_split)
                split(h, wo_raw[:, :], wo_hi[:, par, :], wo_lo[:, par, :], wo_loaded, wo_hi_done, wo_split)

            for b in range(XB):
                inverse_deviation(b, slice(b * BT, (b + 1) * BT))
            split_query_key(0, 0)
            pool.wait_ge(xn_ready, XB)
            pool.memset(acc[:, :, :], 0.0).then_inc(acc_zeroed, 1)
            split_query_key(1, 1)
            split_value_output(0, 0)

            quant_steps = 0

            def quantise(i, start=0, stop=BANK):
                m, k = divmod(PIECE_ORDER[i], FFN_PIECES)
                part = slice(k * BANK + start, k * BANK + stop)
                hi = (k_hi[:, 0, :], w2_hi[:, :, :].rearrange("p f d -> p (f d)"))[m][:, part]
                lo = (k_lo[:, 0, :], w2_lo[:, :, :].rearrange("p f d -> p (f d)"))[m][:, part]
                raw = ffn_raw[:, i % 2, start:stop]
                above, below = tmp[:, 0, start:stop], tmp[:, 1, start:stop]
                if start == 0:
                    pool.wait_ge(piece_loaded[i % 2], 16 * (FFN_PIECES + i // 2 + 1))

                def then(ins):
                    nonlocal quant_steps
                    quant_steps += 1
                    ins.then_inc(quant_step, 1)
                    pool.wait_ge(quant_step, quant_steps)

                then(pool.tensor_scalar(above, raw, half_scale[:, m:m + 1], None, ALU.is_gt))
                then(pool.tensor_scalar(below, raw, neg_half_scale[:, m:m + 1], None, ALU.is_lt))
                then(pool.tensor_tensor(above, above, below, ALU.subtract))
                then(pool.tensor_tensor(above, above, raw, ALU.subtract))
                then(pool.tensor_tensor(below, above, raw, ALU.add))
                then(pool.tensor_copy(hi, below))
                last = pool.tensor_tensor(lo, below, hi.bitcast(F32), ALU.subtract)
                if stop == BANK:
                    last.then_inc(piece_done, 1)
                    pool.wait_ge(piece_done, i + 1)
                else:
                    then(last)

            def weigh_bank(h, u):
                i = BY_POOL.index(u)
                pool.wait_ge(rinv_ready, UNITS * h + (u + 1))
                if i == 0:
                    need(pool, c_added, PE_SUMS * h)
                elif i > 1:
                    pool.wait_ge(weighted_added, ADDS * h + (i - 1))
                pool.tensor_tensor((weighted if i else weighted_sum)[:, ACT_KEYS:TOKENS], probs[:, u % 2, ACT_KEYS:TOKENS],
                                   rinv[:, u % 2:u % 2 + 1].broadcast_to([P, TOKENS - ACT_KEYS]),
                                   ALU.mult).then_inc(bank_weighted, 1)

            def head(h, par, last_but_one=False):
                weigh_bank(h, BY_POOL[0])
                for i in range(1, len(BY_POOL)):
                    if BY_POOL[i] in SHARED:
                        weigh_bank(h, BY_POOL[i])
                        pool.wait_ge(bank_weighted, len(SHARED) * h + SHARED.index(BY_POOL[i]) + 1)
                    elif i == 1:
                        pool.wait_ge(bank_weighted, len(SHARED) * h + 1)
                    pool.wait_ge(weighted_ready, len(BY_POOL) * h + (i + 1))
                    if i > 1:
                        pool.wait_ge(weighted_added, ADDS * h + (i - 1))
                    pool.tensor_tensor(weighted_sum[:, :], weighted[:, :], weighted_sum[:, :],
                                       ALU.add).then_inc(weighted_added, 1)
                    if BY_POOL[i] == 3 and not (isinstance(h, int) and h == 0):
                        pool.wait_ge(c_added, PE_SUMS * h)
                        split_value_output(h, par)
                    if BY_POOL[i] == 9 and not last_but_one:
                        pool.wait_ge(q_ready, 4 * h + 4)
                        split_query_key(h + 2, par)
                    if last_but_one and i in (2, 4):
                        quantise(0, (i // 2 - 1) * CHUNK, (i // 2) * CHUNK)

            head(0, 0)
            head(1, 1)
            with pool.Fori(1, HEADS // 2 - 1) as it:
                head(2 * it, 0)
                head(2 * it + 1, 1)
            pool.wait_ge(thresholds, 3)
            head(LAST - 1, 0, last_but_one=True)
            pool.wait_ge(c_added, PE_SUMS * LAST)
            split_value_output(LAST, LAST % 2)

            pool.wait_ge(s_ready, BANKS * UNITS * LAST)
            for i in range(EARLY, 2 * FFN_PIECES):
                quantise(i)
            sets = XB

            def deviations(tiles):
                nonlocal sets
                inverse_deviation(sets, tiles)
                sets += 1

            def both_norms(b):
                for _ in range(2):
                    deviations(slice(b * BT, (b + 1) * BT))

            def finish(c):
                deviations(slice(2 * c, 2 * c + 2))

            def split_hidden(c):
                for half in range(2):
                    fs = slice(half * FT // 2, (half + 1) * FT // 2)
                    pool.wait_ge(h_hi_done, 2 * c + half + 1)
                    need(pool, f_ready, c - 1)
                    h = hidden[:, c % 2, :].rearrange("p (f n) -> p f n", f=FT)[:, fs, :]
                    pool.tensor_tensor(hid_lo[:, c % 2, fs, :], h, hid_hi[:, c % 2, fs, :].bitcast(F32),
                                       ALU.subtract).then_inc(h_lo_done, 1)

            both_norms(0)
            both_norms(1)
            for c in range(CHUNKS):
                split_hidden(c)
                if c == 1:
                    both_norms(2)
                if c:
                    finish(c - 1)
                if c == 3:
                    both_norms(3)
            finish(CHUNKS - 1)

        @block.tensor
        def _(pe):
            def product(ps, pairs, first=True, last=True):
                n = 3 * len(pairs)
                i = 0
                for ah, al, bh, bl in pairs:
                    for a, b in ((ah, bh), (ah, bl), (al, bh)):
                        ins = pe.matmul(ps, a, b, start=first and i == 0, stop=last and i == n - 1)
                        i += 1
                return ins

            def project(ps, w_h, w_l, cols, chunk):
                toks = slice(chunk * BANK, (chunk + 1) * BANK)
                return product(ps, [(w_h[:, c, cols], w_l[:, c, cols], xt_hi[:, c, toks], xt_lo[:, c, toks])
                                    for c in range(HC)])

            def queries(ps, par, chunk):
                return project(ps, wqk_hi[:, par], wqk_lo[:, par], slice(0, D), chunk)

            def keys(ps, par, chunk):
                return project(ps, wqk_hi[:, par], wqk_lo[:, par], slice(D, 2 * D), chunk)

            pe.wait_ge(const_made, 4)
            for g in range(TILES // 2):
                pe.wait_ge(xn_ready, g // 2 + 1)
                need(pe, xt_lo_done, g - 3)
                for c in range(HC):
                    for t in range(2):
                        ins = pe.transpose(ps_s[:, g % 4, (2 * c + t) * P:(2 * c + t + 1) * P],
                                           xn[:, 2 * g + t, c * P:(c + 1) * P], ident[:, :])
                ins.then_inc(xt_ready, 1)
            pe.wait_ge(wqk_split, 1)
            for c in range(BANKS):
                pe.wait_ge(xt_lo_done, max(2 * c + 2, 4 + c + 1))
                keys(ps_s[:, c, :], 0, c).then_inc(k_ready, 1)
                if c == 0:
                    queries(ps_x[:, X_QUERIES, :], 0, 0).then_inc(q_ready, 1)

            def scores(h, par, r, bank):
                n = UNITS * h + r
                need(pe, exp_done, BANKS * (n - 1) + bank)
                if bank == 0 and r % 4 == 0:
                    pe.wait_ge(q_lo_done, 4 * h + r // 4 + 1)
                if r == 0:
                    pe.wait_ge(k_lo_done, 4 * h + bank + 1)
                qs = slice((r % 4) * P, (r % 4 + 1) * P)
                ks = slice(bank * BANK, (bank + 1) * BANK)
                q = (r // 4) % 2
                product(ps_s[:, score_bank(r, bank), :], [(q_hi[:, q, qs], q_lo[:, q, qs], k_hi[:, par, ks], k_lo[:, par, ks])])\
                    .then_inc(s_ready, 1)

            def sums_over_queries(n, u, stop=False):
                pe.wait_ge(rinv_ready, n + 1)
                for b in range(BANKS):
                    ins = pe.matmul(ps_c[32 * b:32 * b + 1, :], rinv[:, u % 2:u % 2 + 1],
                                    probs[:, u % 2, b * BANK:(b + 1) * BANK], start=u == 0, stop=stop)
                ins.then_inc(c_added, 1)

            def sums_of_weighted(h):
                pe.wait_ge(weighted_added, ADDS * (h + 1))
                for b in range(BANKS):
                    ins = pe.matmul(ps_c[32 * b:32 * b + 1, :], ones[:, 0:1], weighted_sum[:, b * BANK:(b + 1) * BANK],
                                    start=False, stop=True)
                ins.then_inc(c_added, 1)

            def output(y, par, bank):
                vb = (y // 2) % 2
                for s in range(2):
                    ts = slice((y % 2) * CHUNK + s * P, (y % 2) * CHUNK + (s + 1) * P)
                    ins = product(bank[:, s * HID:(s + 1) * HID],
                                  [(v_hi[:, vb, ts], v_lo[:, vb, ts], wo_hi[:, par, :], wo_lo[:, par, :])])
                ins.then_inc(y_ready, 1)

            def values(h, par, c):
                if c == 0:
                    pe.wait_ge(wv_split, h + 1)
                project(ps_x[:, X_VALUES, :], wv_hi[:, par], wv_lo[:, par], slice(0, D), c).then_inc(v_ready, 1)

            def turn_columns(h):
                pe.wait_ge(c_row_done, h + 1)
                pe.wait_ge(exp_done, BANKS * UNITS * HEADS if isinstance(h, int) and h == LAST
                           else BANKS * UNITS * (h + 1) + 3 * BANKS)
                for s in range(BANKS):
                    ins = pe.matmul(ps_s[:, 0, 4 * s:4 * s + 4], c_row[:, s * P:(s + 1) * P],
                                    ident[:, 0:P:32], start=True, stop=True)
                ins.then_inc(c_turned, 1)

            def slot(h, par, r, h0=False, last=False):
                n, c = UNITS * h + r, r // 4
                if r == 4 and not h0:
                    pe.wait_ge(c_col_done, h)
                for bank in range(BANKS):
                    scores(h, par, r, bank)
                if r % 4 == 0:
                    if not h0 and (r > 0 or not isinstance(h, int) or h > 1):
                        pe.wait_ge(y_used, YS * (h - 1) + (2 * c - 1))
                        output((2 * c - 1) % YS, 1 - par if r else par, ps_x[:, X_ROWS, :])
                    if not (last and c == 3):
                        pe.wait_ge(k_lo_done, 4 * HEADS if last else 4 * (h + 1) + c)
                        queries(ps_x[:, X_QUERIES, :], par if c < 3 else 1 - par, (c + 1) % 4).then_inc(q_ready, 1)
                if r % 4 == 1 and not h0:
                    need(pe, y_used, YS * (h - 1) + 2 * c)
                    values(h - 1, 1 - par, c)
                if r % 4 == 2 and not last:
                    pe.wait_ge(q_lo_done, 4 * h + c + 2)
                    if c == 0:
                        pe.wait_ge(wqk_split, h + 2)
                    keys(ps_x[:, X_KEYS, :], 1 - par, c).then_inc(k_ready, 1)
                if r == 3 and not h0:
                    turn_columns(h - 1)
                if r % 4 == 3 and not h0:
                    pe.wait_ge(v_lo_done, 4 * (h - 1) + c + 1)
                    if c == 0:
                        pe.wait_ge(wo_split, h)
                    output(2 * c, 1 - par, ps_x[:, X_ROWS, :])

                if r == 1 and h0:
                    pe.wait_ge(c_cleared, 1)
                elif r == 1:
                    pe.wait_ge(c_row_done, h)
                if not (h0 and r == 0) and (last or r - 1 not in BY_POOL):
                    sums_over_queries(n - 1, (r - 1) % UNITS)
                if r == 0 and not h0:
                    sums_of_weighted(h - 1)

                if h0 and r == 12:
                    pe.wait_ge(abs_done, 2 * FFN_PIECES + 2)
                    pe.matmul(ps_x[:, X_VALUES, 0:2], ones[:, :], abs_sum[:, :], start=True, stop=True)\
                        .then_inc(scale_ready, 1)
                if h0 and r == 15:
                    pe.wait_ge(thresholds, 1)

            def head(h, par, h0=False, last=False):
                for r in range(UNITS):
                    slot(h, par, r, h0, last)

            head(0, 0, h0=True)
            head(1, 1)
            with pe.Fori(1, HEADS // 2 - 1) as it:
                head(2 * it, 0)
                head(2 * it + 1, 1)
            head(LAST - 1, 0)
            head(LAST, 1, last=True)


            def turn_block_input(b):
                pe.wait_ge(xn_ready, XB + b + 1)
                for g in range(2 * b, 2 * b + 2):
                    need(pe, tr_lo_done, g - 1)
                    for c in range(HC):
                        for t in range(2):
                            ins = pe.transpose(ps_turned[g % 2][:, (2 * c + t) * P:(2 * c + t + 1) * P],
                                               x_stage[:, b % 2, (2 * g + t) % BT, c * P:(c + 1) * P], ident[:, :])
                    ins.then_inc(tr_ready, 1)

            def up(c):
                pe.wait_ge(tr_lo_done, c + 1)
                toks = slice(c * CHUNK, (c + 1) * CHUNK)
                for f in range(FT):
                    if f % 2 == 0:
                        need(pe, gelu_done, FT * (c - 1) + f + 2)
                    fs = slice(f * P, (f + 1) * P)
                    product(ps_s[:, f // 2, (f % 2) * CHUNK:(f % 2 + 1) * CHUNK],
                            [(w1_hi[:, k, fs], w1_lo[:, k, fs], xt_hi[:, k, toks], xt_lo[:, k, toks]) for k in range(HC)])\
                        .then_inc(h_ready, 1)

            def down(c):
                pe.wait_ge(h_lo_done, 2 * c + 2)
                need(pe, f_used, c - 1)
                for t in range(2):
                    ts = slice(t * P, (t + 1) * P)
                    ins = product(ps_f[c % 2][:, t * HID:(t + 1) * HID],
                                  [(hid_hi[:, c % 2, f, ts], hid_lo[:, c % 2, f, ts], w2_hi[:, f, :], w2_lo[:, f, :])
                                   for f in range(FT)])
                ins.then_inc(f_ready, 1)

            def last_values(c):
                pe.wait_ge(y_used, YS * LAST + max(2 * c - 1, 0))
                values(LAST, LAST % 2, c)

            def last_rows(c):
                pe.wait_ge(v_lo_done, 4 * LAST + c + 1)
                if c == 0:
                    pe.wait_ge(wo_split, HEADS)
                output(2 * c, LAST % 2, ps_x[:, X_ROWS, :])
                pe.wait_ge(y_used, YS * LAST + 2 * c)
                output(2 * c + 1, LAST % 2, ps_s[:, SPARE, :])

            pe.wait_ge(y_used, YS * LAST - 1)
            output(YS - 1, (LAST - 1) % 2, ps_x[:, X_ROWS, :])
            sums_over_queries(UNITS * HEADS - 1, UNITS - 1, stop=True)
            last_values(0)
            turn_columns(LAST)
            last_rows(0)
            last_values(1)
            last_rows(1)
            last_values(2)
            turn_block_input(0)
            pe.wait_ge(piece_done, EARLY + FFN_PIECES)
            up(0)
            last_rows(2)
            up(1)
            last_values(3)
            turn_block_input(1)
            last_rows(3)
            pe.wait_ge(piece_done, 2 * FFN_PIECES)
            pe.wait_ge(y_used, YS * HEADS)
            down(0)
            up(2)
            for c in range(2, CHUNKS):
                if c % 2 and (c + 1) // 2 < XB:
                    turn_block_input((c + 1) // 2)
                down(c - 1)
                if c + 1 < CHUNKS:
                    up(c + 1)
            down(CHUNKS - 1)

        @block.scalar
        def _(act):
            for g in range(TILES // 2):
                act.wait_ge(xt_ready, g + 1)
                act.activation(xt_hi[:, :, g * CHUNK:(g + 1) * CHUNK],
                               ps_s[:, g % 4, :].rearrange("p (c n) -> p c n", c=HC), ACT.Copy).then_inc(xt_hi_done, 1)

            def keys(h, par, c, src):
                act.wait_ge(k_ready, 4 * h + c + 1)
                act.activation(k_hi[:, par, c * BANK:(c + 1) * BANK], src, ACT.Copy).then_inc(k_hi_done, 1)

            def queries(h, c):
                act.wait_ge(q_ready, 4 * h + c + 1)
                act.activation(q_hi[:, c % 2, :], ps_x[:, X_QUERIES, :], ACT.Copy, scale=SCALE).then_inc(q_hi_done, 1)

            for c in range(BANKS):
                keys(0, 0, c, ps_s[:, c, :])
                if c == 0:
                    queries(0, 0)

            def exp_unit(n, r):
                act.wait_ge(max_ready, n + 1)
                for b in (1, 2, 3, 0):
                    act.activation(probs[:, r % 2, b * BANK:(b + 1) * BANK], ps_s[:, score_bank(r, b), :], ACT.Exp,
                                   bias=negmax[:, r % 2:r % 2 + 1], scale=1.0,
                                   accum_out=rowsum[:, r % 2, b:b + 1]).then_inc(exp_done, 1)

            def weigh(h, u):
                i = BY_POOL.index(u)
                act.wait_ge(rinv_ready, UNITS * h + (u + 1))
                if i > 1:
                    act.wait_ge(weighted_added, ADDS * h + (i - 1))
                keys = slice(0, ACT_KEYS if u in SHARED else TOKENS)
                act.activation((weighted if i else weighted_sum)[:, keys], probs[:, u % 2, keys], ACT.Copy,
                               scale=rinv[:, u % 2:u % 2 + 1]).then_inc(weighted_ready, 1)

            def copy_row(h, sums):
                act.wait_ge(c_added, sums)
                need(act, c_turned, h)
                act.activation(c_row[:, :], ps_c[:, :], ACT.Copy).then_inc(c_row_done, 1)

            def values(h, c):
                act.wait_ge(v_ready, 4 * h + c + 1)
                need(act, y_ready, YS * h + (2 * c - 2))
                act.activation(v_hi[:, c % 2, :], ps_x[:, X_VALUES, :], ACT.Copy).then_inc(v_hi_done, 1)

            def slot(h, par, r, h0=False, last=False):
                c = r // 4
                if r == 1 and not h0:
                    copy_row(h - 1, PE_SUMS * h)
                if r % 4 == 2 and not h0:
                    values(h - 1, c)
                if not last and r - 2 in BY_POOL:
                    weigh(h, r - 2)
                    if r - 2 in SHARED:
                        act.wait_ge(bank_weighted, len(SHARED) * h + SHARED.index(r - 2) + 1)
                    act.wait_ge(weighted_ready, len(BY_POOL) * h + BY_POOL.index(r - 2) + 1)
                exp_unit(UNITS * h + r, r)

            def head(h, par, h0=False, last=False):
                for r in range(UNITS):
                    slot(h, par, r, h0, last)

            head(0, 0, h0=True)
            head(1, 1)
            with act.Fori(1, HEADS // 2 - 1) as it:
                head(2 * it, 0)
                head(2 * it + 1, 1)
            head(LAST - 1, 0)
            head(LAST, 1, last=True)
            copy_row(LAST, PE_SUMS * LAST + UNITS)
            for c in range(3):
                values(LAST, c)

            act.wait_ge(consts_loaded, 32)

            def split_turned(g):
                act.wait_ge(tr_ready, g + 1)
                act.activation(xt_hi[:, :, g * CHUNK:(g + 1) * CHUNK],
                               ps_turned[g % 2].rearrange("p (c n) -> p c n", c=HC), ACT.Copy).then_inc(tr_hi_done, 1)

            split_turned(0)
            split_turned(1)
            for c in range(CHUNKS):
                need(act, h_lo_done, 2 * c - 2)
                for f in range(FT):
                    if f % 2 == 0:
                        act.wait_ge(h_ready, FT * c + f + 2)
                    act.activation(hidden[:, c % 2, f * CHUNK:(f + 1) * CHUNK],
                                   ps_s[:, f // 2, (f % 2) * CHUNK:(f % 2 + 1) * CHUNK], ACT.Gelu,
                                   bias=b1[:, f:f + 1], scale=1.0).then_inc(gelu_done, 1)
                    if f % (FT // 2) == FT // 2 - 1:
                        act.wait_ge(gelu_done, FT * c + f + 1)
                        need(act, f_ready, c - 1)
                        half = slice(f + 1 - FT // 2, f + 1)
                        act.activation(hid_hi[:, c % 2, half, :],
                                       hidden[:, c % 2, half.start * CHUNK:half.stop * CHUNK]
                                       .rearrange("p (f n) -> p f n", n=CHUNK), ACT.Copy).then_inc(h_hi_done, 1)
                if c == 1:
                    values(LAST, 3)
                if c % 2 and (c + 1) // 2 < XB:
                    split_turned(c + 1)
                    split_turned(c + 2)

        @block.vector
        def _(dve):
            ln_steps = 0

            def variances(sets, tiles, src, wait_src=None):
                nonlocal ln_steps
                for i, t in enumerate(tiles):
                    dve.bn_stats(stats[:, i, :], src(t)).then_inc(ln_step, 1)
                    ln_steps += 1
                first = ln_steps - len(tiles)
                for i, t in enumerate(tiles):
                    dve.wait_ge(ln_step, first + i + 1)
                    dve.bn_aggr(mv[:, t, :], stats[:, i, :]).then_inc(ln_step, 1)
                    ln_steps += 1
                dve.wait_ge(ln_step, ln_steps)
                a, b = tiles[0], tiles[-1] + 1
                dve.tensor_scalar(var_eps[:, a:b], mv[:, a:b, 1], LN_EPS, None, ALU.add).then_inc(ln_var, 1)

            def normalise(dst, src, t):
                return dve.tensor_scalar(dst, src, mv[:, t, 0:1], rstd[:, t:t + 1], ALU.subtract, ALU.mult)

            batch = [list(range(b * BT, (b + 1) * BT)) for b in range(XB)]

            def normalise_input(b):
                dve.wait_ge(ln_rstd, b + 1)
                for t in batch[b]:
                    ins = normalise(xn[:, t, :], acc[:, t, :], t)
                ins.then_inc(xn_ready, 1)

            for b in range(XB):
                dve.wait_ge(x_loaded[b], 16)
                if b:
                    dve.wait_ge(ln_step, ln_steps)
                variances(b, batch[b], lambda t: acc[:, t, :])
                if b:
                    normalise_input(b - 1)
            normalise_input(XB - 1)

            for g in range(TILES // 2):
                dve.wait_ge(xt_hi_done, g + 1)
                hi = xt_hi[:, :, g * CHUNK:(g + 1) * CHUNK]
                dve.tensor_tensor(xt_lo[:, :, g * CHUNK:(g + 1) * CHUNK],
                                  ps_s[:, g % 4, :].rearrange("p (c n) -> p c n", c=HC), hi.bitcast(F32),
                                  ALU.subtract).then_inc(xt_lo_done, 1)

            dve.memset(ps_c[:, :], 0.0).then_inc(c_cleared, 1)

            def keys_lo(h, par, c, src):
                dve.wait_ge(k_hi_done, 4 * h + c + 1)
                ks = slice(c * BANK, (c + 1) * BANK)
                dve.tensor_tensor(k_lo[:, par, ks], src, k_hi[:, par, ks].bitcast(F32), ALU.subtract).then_inc(k_lo_done, 1)

            def keys(h, par, c, src):
                dve.wait_ge(k_ready, 4 * h + c + 1)
                dve.tensor_copy(k_hi[:, par, c * BANK:(c + 1) * BANK], src).then_inc(k_hi_done, 1)
                keys_lo(h, par, c, src)

            def queries_lo(h, c):
                dve.wait_ge(q_hi_done, 4 * h + c + 1)
                dve.scalar_tensor_tensor(out=q_lo[:, c % 2, :], in0=ps_x[:, X_QUERIES, :], scalar=SCALE,
                                         in1=q_hi[:, c % 2, :].bitcast(F32), op0=ALU.mult, op1=ALU.subtract)\
                    .then_inc(q_lo_done, 1)

            def queries(h, c):
                dve.wait_ge(q_ready, 4 * h + c + 1)
                dve.tensor_scalar(q_hi[:, c % 2, :], ps_x[:, X_QUERIES, :], SCALE, None, ALU.mult).then_inc(q_hi_done, 1)
                queries_lo(h, c)

            for c in range(BANKS):
                keys_lo(0, 0, c, ps_s[:, c, :])
                if c == 0:
                    queries_lo(0, 0)

            def sum_magnitudes(i):
                dve.wait_ge(piece_loaded[i % 2], 16 * (i // 2 + 1))
                dve.tensor_reduce(abs_piece[:, i:i + 1], ffn_raw[:, i % 2, :], AX_X, ALU.add,
                                  apply_absolute_value=True).then_inc(abs_done, 1)

            def sum_pieces():
                dve.wait_ge(abs_done, 2 * FFN_PIECES)
                for m in range(2):
                    dve.tensor_reduce(abs_sum[:, m:m + 1], abs_piece[:, m * FFN_PIECES:(m + 1) * FFN_PIECES], AX_X,
                                      ALU.add).then_inc(abs_done, 1)

            def make_thresholds():
                dve.wait_ge(scale_ready, 1)
                dve.tensor_scalar(scale[:, :], ps_x[:, X_VALUES, 0:2], 1.0 / (HID * DFF), QUANT_EPS, ALU.mult, ALU.max)\
                    .then_inc(thresholds, 1)
                dve.wait_ge(thresholds, 1)
                dve.tensor_scalar(half_scale[:, :], scale[:, :], 0.5, None, ALU.mult).then_inc(thresholds, 1)
                dve.tensor_scalar(neg_half_scale[:, :], scale[:, :], -0.5, None, ALU.mult).then_inc(thresholds, 1)

            def bank_max(n, r, bank):
                dve.wait_ge(s_ready, 4 * n + bank + 1)
                dve.tensor_reduce(qmax[:, r % 2, bank:bank + 1], ps_s[:, score_bank(r, bank), :], AX_X, ALU.max).then_inc(qmax_done, 1)

            def row_max(n, r):
                dve.wait_ge(qmax_done, 4 * n + BANKS)
                dve.tensor_reduce(negmax[:, r % 2:r % 2 + 1], qmax[:, r % 2, :], AX_X, ALU.max,
                                  negate=True).then_inc(max_ready, 1)

            def row_sum(n, u):
                dve.wait_ge(exp_done, BANKS * (n + 1))
                dve.tensor_reduce(total[:, u % 2:u % 2 + 1], rowsum[:, u % 2, :], AX_X, ALU.add).then_inc(sum_step, 1)
                dve.wait_ge(sum_step, n + 1)
                dve.reciprocal(rinv[:, u % 2:u % 2 + 1], total[:, u % 2:u % 2 + 1]).then_inc(rinv_ready, 1)

            def add_rows(h, y, rows=ps_x[:, X_ROWS, :]):
                dve.wait_ge(y_ready, YS * h + y + 1)
                if y == 0:
                    dve.wait_ge(c_col_done, h + 1)
                    dve.wait_ge(acc_zeroed, 1)
                need(dve, y_used, YS * h + y)
                for s in range(2):
                    tile = 2 * y + s
                    a, b = tile % BANKS, tile // BANKS
                    ins = dve.scalar_tensor_tensor(out=acc[:, tile, :], in0=rows[:, s * HID:(s + 1) * HID],
                                                   scalar=c_col[:, a, b:b + 1], in1=acc[:, tile, :],
                                                   op0=ALU.mult, op1=ALU.add)
                ins.then_inc(y_used, 1)

            def values_lo(h, c):
                dve.wait_ge(v_hi_done, 4 * h + c + 1)
                dve.tensor_tensor(v_lo[:, c % 2, :], ps_x[:, X_VALUES, :], v_hi[:, c % 2, :].bitcast(F32),
                                  ALU.subtract).then_inc(v_lo_done, 1)

            def copy_columns(h):
                dve.wait_ge(c_turned, h + 1)
                need(dve, y_used, YS * h)
                dve.tensor_copy(c_col[:, :, :], ps_s[:, 0, 0:16].rearrange("p (a b) -> p a b", a=BANKS))\
                    .then_inc(c_col_done, 1)

            def slot(h, par, r, h0=False, last=False):
                n, c = UNITS * h + r, r // 4
                sum_now = (last or r - 1 not in BY_POOL) and not (h0 and r == 0)
                sum_later = not sum_now and r > 0
                rows = r % 4 == 0 and not h0 and (r > 0 or not isinstance(h, int) or h > 1)
                if rows:
                    add_rows(h - 1 if r else h - 2, (2 * c - 2) % YS)
                bank_max(n, r, 0)
                bank_max(n, r, 1)
                bank_max(n, r, 2)
                if sum_now:
                    row_sum(n - 1, (r - 1) % UNITS)
                bank_max(n, r, 3)
                row_max(n, r)
                if sum_later:
                    row_sum(n - 1, (r - 1) % UNITS)
                if rows:
                    add_rows(h - 1 if r else h - 2, (2 * c - 1) % YS)
                if r == 3 and not h0:
                    copy_columns(h - 1)
                if r % 4 == 1 and not (last and c == 3):
                    queries(h, c + 1)
                if r % 4 == 2 and not h0:
                    values_lo(h - 1, c)
                if r % 4 == 3 and not last:
                    keys(h + 1, 1 - par, c, ps_x[:, X_KEYS, :])

            def head(h, par, h0=False, last=False):
                for r in range(UNITS):
                    slot(h, par, r, h0, last)
                    if h0 and 2 <= r < 2 + 2 * FFN_PIECES:
                        sum_magnitudes(r - 2)
                    if h0 and r == 2 + 2 * FFN_PIECES:
                        sum_pieces()
                    if h0 and r == 12:
                        make_thresholds()

            head(0, 0, h0=True)
            head(1, 1)
            with dve.Fori(1, HEADS // 2 - 1) as it:
                head(2 * it, 0)
                head(2 * it + 1, 1)
            head(LAST - 1, 0)
            head(LAST, 1, last=True)

            def pair(y):
                add_rows(LAST, y)
                add_rows(LAST, y + 1, ps_s[:, SPARE, :])

            add_rows(LAST - 1, YS - 2)
            row_sum(UNITS * HEADS - 1, UNITS - 1)
            add_rows(LAST - 1, YS - 1)
            values_lo(LAST, 0)
            copy_columns(LAST)
            pair(0)

            sets = XB

            def deviations(tiles, src):
                nonlocal sets
                dve.wait_ge(ln_step, ln_steps)
                variances(sets, tiles, src)
                sets += 1
                dve.wait_ge(ln_rstd, sets)

            def then(ins):
                nonlocal local_steps
                local_steps += 1
                ins.then_inc(local_step, 1)

            def settled():
                dve.wait_ge(local_step, local_steps)

            local_steps = 0

            def attention_stats(b):
                nonlocal sets
                dve.wait_ge(y_used, YS * LAST + 2 * (b + 1))
                dve.wait_ge(ln_step, ln_steps)
                variances(sets, batch[b], lambda t: acc[:, t, :])
                sets += 1

            def attention_norm(b):
                nonlocal sets
                dve.wait_ge(ln_rstd, sets)
                for t in batch[b]:
                    then(normalise(acc[:, t, :], acc[:, t, :], t))
                dve.wait_ge(x_again[b % 2], 16 * (b // 2 + 1))
                settled()
                for t in batch[b]:
                    then(dve.tensor_tensor(acc[:, t, :], acc[:, t, :], x_stage[:, b % 2, t % BT, :], ALU.add))
                settled()
                variances(sets, batch[b], lambda t: acc[:, t, :])
                sets += 1

            def input_norm(b):
                dve.wait_ge(ln_rstd, sets)
                for t in batch[b]:
                    ins = normalise(x_stage[:, b % 2, t % BT, :], acc[:, t, :], t)
                ins.then_inc(xn_ready, 1)

            def split_turned(g):
                dve.wait_ge(tr_hi_done, g + 1)
                toks = slice(g * CHUNK, (g + 1) * CHUNK)
                dve.tensor_tensor(xt_lo[:, :, toks], ps_turned[g % 2].rearrange("p (c n) -> p c n", c=HC),
                                  xt_hi[:, :, toks].bitcast(F32), ALU.subtract).then_inc(tr_lo_done, 1)

            def finish(c):
                dve.wait_ge(f_ready, c + 1)
                need(dve, rows_done, c)
                ffn = tmp[:, 0, :].rearrange("p (t d) -> p t d", t=2)
                for t in range(2):
                    ins = dve.tensor_tensor(ffn[:, t, :], ps_f[c % 2][:, t * HID:(t + 1) * HID], b2[:, :], ALU.add)
                ins.then_inc(f_used, 1)
                dve.wait_ge(f_used, c + 1)
                deviations([2 * c, 2 * c + 1], lambda t: ffn[:, t % 2, :])
                for t in range(2):
                    then(normalise(ffn[:, t, :], ffn[:, t, :], 2 * c + t))
                settled()
                tiles = slice(2 * c, 2 * c + 2)
                dve.tensor_tensor(acc[:, tiles, :], acc[:, tiles, :], ffn, ALU.add).then_inc(rows_done, 1)

            attention_stats(0)
            values_lo(LAST, 1)
            attention_norm(0)
            pair(2)
            input_norm(0)
            attention_stats(1)
            split_turned(0)
            split_turned(1)
            values_lo(LAST, 2)
            attention_norm(1)
            input_norm(1)
            pair(4)
            values_lo(LAST, 3)
            attention_stats(2)
            pair(6)
            split_turned(2)
            split_turned(3)
            attention_norm(2)
            input_norm(2)
            dve.wait_ge(consts_loaded, 32)
            for c in range(CHUNKS):
                if c % 2 and 1 < (c + 1) // 2 < XB:
                    split_turned(c + 1)
                    split_turned(c + 2)
                if c:
                    finish(c - 1)
                if c == 3:
                    attention_stats(3)
                    attention_norm(3)
                    input_norm(3)
            finish(CHUNKS - 1)


def kernel(L0_attn_x, L0_attn_w_qkv, L0_attn_w_o, L0_ffn_w1, L0_ffn_b1, L0_ffn_w2, L0_ffn_b2):
    import numpy as np
    import concourse.bacc as bacc
    from concourse.bass_utils import run_bass_kernel_spmd

    x = np.asarray(L0_attn_x)
    batch, tokens, hid = x.shape
    d = P
    heads = L0_attn_w_o.shape[0] // d
    dff = L0_ffn_w1.shape[0]
    hc = hid // P
    w_qkv = np.asarray(L0_attn_w_qkv).reshape(hc, P, 3, heads, d)
    arrays = {
        "x": x.reshape(batch * tokens, hid),
        "w_qk": w_qkv[:, :, 0:2].transpose(3, 1, 0, 2, 4).reshape(heads, P, hc, 2 * d),
        "w_v": w_qkv[:, :, 2].transpose(2, 1, 0, 3),
        "w_o": np.asarray(L0_attn_w_o).reshape(heads, d, hid),
        "w1": np.asarray(L0_ffn_w1).T.reshape(hc, P, dff).transpose(1, 0, 2),
        "b1": np.asarray(L0_ffn_b1).reshape(dff // P, P).T,
        "w2": np.asarray(L0_ffn_w2).T.reshape(dff // P, P, hid).transpose(1, 0, 2),
        "b2": np.asarray(L0_ffn_b2),
    }
    arrays = {f"in_{k}": np.ascontiguousarray(v) for k, v in arrays.items()}
    nc = bacc.Bacc("TRN2", target_bir_lowering=False, num_devices=1)
    ins = [nc.dram_tensor(k, v.shape, mybir.dt.from_np(v.dtype), kind="ExternalInput").ap() for k, v in arrays.items()]
    out = nc.dram_tensor("out", (batch * tokens, hid), F32, kind="ExternalOutput").ap()
    sandwich_block(nc, *ins, out)
    result = run_bass_kernel_spmd(nc, [arrays], core_ids=[0])
    return result.results[0]["out"].reshape(batch, tokens, hid)
```
